# Optimizing a Trainium2 kernel written in Bass

```python
import numpy as np
import jax
import jax.numpy as jnp

def _softmax(x, axis=-1):
    return jax.nn.softmax(x, axis=axis)

def _gelu(x):
    return jax.nn.gelu(x, approximate=True)

def _silu(x):
    return jax.nn.silu(x)

def _sigmoid(x):
    return jax.nn.sigmoid(x)

def _layernorm(x, axis=-1, eps=1e-05):
    m = jnp.mean(x, axis=axis, keepdims=True)
    v = jnp.var(x, axis=axis, keepdims=True)
    return (x - m) / jnp.sqrt(v + eps)

def _scatter_add(tgt, idx, src, axis=0):
    return tgt.at[idx].add(src)

def _segment_sum(src, seg, n):
    return jax.ops.segment_sum(src, seg, n)
kernel_name = 'mk_seq_preln_d1_jaxref_r8_d156d5'

def setup_inputs(seed: int=0):
    np.random.seed(seed)
    _w = jnp.asarray

    def _L0_attn_setup():
        import jax, jax.numpy as jnp
        import numpy as np
        D_MODEL = 128
        D_HEAD = 64
        N_HEADS = 16
        STATE = 64
        D_INNER = D_HEAD * N_HEADS
        B, T = (4, 256)
        LN_EPS = 1e-05

        def _linear_params(key, fan_out, fan_in):
            k1, k2 = jax.random.split(key)
            s = 1.0 / np.sqrt(fan_in)
            W = jax.random.uniform(k1, (fan_out, fan_in), jnp.float32, -s, s)
            b = jax.random.uniform(k2, (fan_out,), jnp.float32, -s, s)
            return (W, b)

        def _layer_norm(x, gamma, beta):
            mu = jnp.mean(x, axis=-1, keepdims=True)
            var = jnp.mean(jnp.square(x - mu), axis=-1, keepdims=True)
            return (x - mu) * jax.lax.rsqrt(var + LN_EPS) * gamma + beta
        key = jax.random.key(seed)
        ks = jax.random.split(key, 8)
        WQ, bQ = _linear_params(ks[0], D_INNER, D_MODEL)
        WK, bK = _linear_params(ks[1], D_INNER, D_MODEL)
        WV, bV = _linear_params(ks[2], D_INNER, D_MODEL)
        WO, bO = _linear_params(ks[3], D_MODEL, D_INNER)
        Wg, bg = _linear_params(ks[4], D_INNER, D_MODEL)
        alpha_logit = jax.random.normal(ks[5], (N_HEADS, STATE), jnp.float32) * 0.1
        ln_gamma = jnp.ones((D_MODEL,), jnp.float32)
        ln_beta = jnp.zeros((D_MODEL,), jnp.float32)
        x = jax.random.normal(ks[6], (B, T, D_MODEL), jnp.float32)
        return {'x': x, 'WQ': WQ, 'bQ': bQ, 'WK': WK, 'bK': bK, 'WV': WV, 'bV': bV, 'WO': WO, 'bO': bO, 'Wg': Wg, 'bg': bg, 'alpha_logit': alpha_logit, 'ln_gamma': ln_gamma, 'ln_beta': ln_beta}
    _L0_attn_in = _L0_attn_setup()

    def _L0_ffn_setup():
        import jax, jax.numpy as jnp
        import numpy as np
        B, T, D = (2, 256, 128)
        E, DFF, TOPK = (8, 512, 2)
        TEMPERATURE = 1.0
        key = jax.random.key(seed)
        k_x, k_w1, k_w2, k_r = jax.random.split(key, 4)
        x = jax.random.normal(k_x, (B, T, D), dtype=jnp.float32)
        W1 = jax.random.normal(k_w1, (E, DFF, D), dtype=jnp.float32) * 0.02
        W2 = jax.random.normal(k_w2, (E, D, DFF), dtype=jnp.float32) * 0.02
        Wr = jax.random.normal(k_r, (E, D), dtype=jnp.float32) * 0.02
        return {'x': x, 'W1': W1, 'W2': W2, 'Wr': Wr}
    _L0_ffn_in = _L0_ffn_setup()
    _d = {'L0_attn_x': _L0_attn_in['x'], 'L0_attn_WQ': _L0_attn_in['WQ'], 'L0_attn_bQ': _L0_attn_in['bQ'], 'L0_attn_WK': _L0_attn_in['WK'], 'L0_attn_bK': _L0_attn_in['bK'], 'L0_attn_WV': _L0_attn_in['WV'], 'L0_attn_bV': _L0_attn_in['bV'], 'L0_attn_WO': _L0_attn_in['WO'], 'L0_attn_bO': _L0_attn_in['bO'], 'L0_attn_Wg': _L0_attn_in['Wg'], 'L0_attn_bg': _L0_attn_in['bg'], 'L0_attn_alpha_logit': _L0_attn_in['alpha_logit'], 'L0_attn_ln_gamma': _L0_attn_in['ln_gamma'], 'L0_attn_ln_beta': _L0_attn_in['ln_beta'], 'L0_ffn_W1': _L0_ffn_in['W1'], 'L0_ffn_W2': _L0_ffn_in['W2'], 'L0_ffn_Wr': _L0_ffn_in['Wr']}
    _x0 = _d['L0_attn_x']
    _d['L0_attn_x'] = jax.random.normal(jax.random.fold_in(jax.random.key(seed), 1), (8, 256, 128), dtype=_x0.dtype)
    del _x0
    return _d

def reference(L0_attn_x, L0_attn_WQ, L0_attn_bQ, L0_attn_WK, L0_attn_bK, L0_attn_WV, L0_attn_bV, L0_attn_WO, L0_attn_bO, L0_attn_Wg, L0_attn_bg, L0_attn_alpha_logit, L0_attn_ln_gamma, L0_attn_ln_beta, L0_ffn_W1, L0_ffn_W2, L0_ffn_Wr):

    def _L0_attn_ref(x, WQ, bQ, WK, bK, WV, bV, WO, bO, Wg, bg, alpha_logit, ln_gamma, ln_beta):
        import jax, jax.numpy as jnp
        import numpy as np
        D_MODEL = 128
        D_HEAD = 64
        N_HEADS = 16
        STATE = 64
        D_INNER = D_HEAD * N_HEADS
        B, T = (4, 256)
        LN_EPS = 1e-05

        def _linear_params(key, fan_out, fan_in):
            k1, k2 = jax.random.split(key)
            s = 1.0 / np.sqrt(fan_in)
            W = jax.random.uniform(k1, (fan_out, fan_in), jnp.float32, -s, s)
            b = jax.random.uniform(k2, (fan_out,), jnp.float32, -s, s)
            return (W, b)

        def _layer_norm(x, gamma, beta):
            mu = jnp.mean(x, axis=-1, keepdims=True)
            var = jnp.mean(jnp.square(x - mu), axis=-1, keepdims=True)
            return (x - mu) * jax.lax.rsqrt(var + LN_EPS) * gamma + beta
        batch, seq_len, _ = x.shape
        residual = x
        xn = _layer_norm(x, ln_gamma, ln_beta)
        Q = (xn @ WQ.T + bQ).reshape(batch, seq_len, N_HEADS, D_HEAD)
        K = (xn @ WK.T + bK).reshape(batch, seq_len, N_HEADS, D_HEAD)
        V = (xn @ WV.T + bV).reshape(batch, seq_len, N_HEADS, D_HEAD)
        gate = jax.nn.silu(xn @ Wg.T + bg).reshape(batch, seq_len, N_HEADS, D_HEAD)
        alpha = jax.nn.sigmoid(alpha_logit)
        Qs = Q[..., :STATE]
        Ks = K[..., :STATE]

        def step(h, qkv):
            q, k, v = qkv
            h = alpha[None, :, :, None] * h + k[:, :, :, None] * v[:, :, None, :]
            o = jnp.einsum('bhi,bhij->bhj', q, h)
            return (h, o)
        h0 = jnp.zeros((batch, N_HEADS, STATE, D_HEAD), x.dtype)
        qkv_t = (jnp.moveaxis(Qs, 1, 0), jnp.moveaxis(Ks, 1, 0), jnp.moveaxis(V, 1, 0))
        _, o = jax.lax.scan(step, h0, qkv_t)
        o = jnp.moveaxis(o, 0, 1)
        o = o * gate
        y = o.reshape(batch, seq_len, D_INNER) @ WO.T + bO
        return residual + y

    def _L0_ffn_ref(x, W1, W2, Wr):
        import jax, jax.numpy as jnp
        import numpy as np
        B, T, D = (2, 256, 128)
        E, DFF, TOPK = (8, 512, 2)
        TEMPERATURE = 1.0
        logits = jnp.einsum('btd,ed->bte', x, Wr)
        probs = jax.nn.softmax(logits / TEMPERATURE, axis=-1)
        topk_vals, topk_idx = jax.lax.top_k(probs, TOPK)
        router_weights = topk_vals / topk_vals.sum(-1, keepdims=True)
        one_hot = jax.nn.one_hot(topk_idx, E, dtype=x.dtype)
        gate = jnp.einsum('btk,btke->bte', router_weights, one_hot)
        h = jax.nn.silu(jnp.einsum('btd,efd->btef', x, W1))
        y = jnp.einsum('btef,edf->bted', h, W2)
        out = jnp.einsum('bte,bted->btd', gate, y)
        return out
    x = L0_attn_x
    x = x + _L0_attn_ref(_layernorm(x, axis=-1), L0_attn_WQ, L0_attn_bQ, L0_attn_WK, L0_attn_bK, L0_attn_WV, L0_attn_bV, L0_attn_WO, L0_attn_bO, L0_attn_Wg, L0_attn_bg, L0_attn_alpha_logit, L0_attn_ln_gamma, L0_attn_ln_beta)
    x = x + _L0_ffn_ref(_layernorm(x, axis=-1), L0_ffn_W1, L0_ffn_W2, L0_ffn_Wr)
    return x

_drawn_inputs = setup_inputs


def setup_inputs(seed=0):
    import zlib

    import numpy as np

    out = dict(_drawn_inputs(seed))
    spreads = {'L0_attn_ln_gamma': (1.0, 0.2), 'L0_attn_ln_beta': (0.0, 0.1)}
    factors = {'L0_attn_bQ': 3.479,
     'L0_attn_bK': 3.403,
     'L0_attn_bV': 3.353,
     'L0_attn_bO': 6.039,
     'L0_attn_bg': 3.443,
     'L0_attn_alpha_logit': 7.671,
     'L0_ffn_W1': 3.055,
     'L0_ffn_W2': 2.959,
     'L0_ffn_Wr': 3.474}
    for name, (base, spread) in spreads.items():
        noise = np.random.default_rng([zlib.crc32(name.encode()), seed]).standard_normal(out[name].shape)
        drawn = base * np.exp(spread * noise) if base else spread * noise
        out[name] = jnp.asarray(drawn.astype(out[name].dtype))
    for name, factor in factors.items():
        out[name] = (out[name] * factor).astype(out[name].dtype)
    return out
```

```python
from contextlib import ExitStack

import concourse.bass as bass
from concourse import mybir

ALU = mybir.AluOpType
ACT = mybir.ActivationFunctionType
F32 = mybir.dt.float32
F32R = mybir.dt.float32r
I8 = mybir.dt.int8
I32 = mybir.dt.int32
AX = mybir.AxisListType

P = 128
SEQ = 256
D = 128
HEADS, DH = 16, 64
PAIRS = HEADS // 2
CH = HEADS * DH
E, DFF = 8, 512
FB = DFF // P
EPS = 1e-5
GT = 512
LOGIT_MIN = -3.5
LEVELS = [16, 8, 4, 2, 1]
MID, S32, S64, S128 = 0, SEQ, SEQ + SEQ // 2, 2 * SEQ
VER = 5 * SEQ // 2
NEG = -3.0e38


def build(nc, x, w_in, w_out, b_in, b_v, cols, alpha, alpha_row, w1, w2, w_router, out):
    T = x.shape[0]
    NT = T // P
    G = T // GT
    TG = GT // P
    NB = GT // SEQ

    outer = ExitStack()
    with outer:
        def sb(name, shape, dt=F32, ctx=outer):
            return ctx.enter_context(nc.sbuf_tensor(name, shape, dt))

        def sem(name, ctx=outer):
            return ctx.enter_context(nc.semaphore(name))

        x_all = sb("x_all", [P, NT, D])
        u_all = sb("u_all", [P, NT, D])
        stats = sb("stats", [P, NT, 6])
        mv = sb("mv", [P, NT, 2])
        std = sb("std", [P, NT])
        rstd = sb("rstd", [P, NT])
        eps_col = sb("eps_col", [P, 1])
        ident = sb("ident", [P, P])
        w1_hi = sb("w1_hi", [P, E, FB, P], F32R)
        w1_lo = sb("w1_lo", [P, E, FB, P], F32R)
        w2_hi = sb("w2_hi", [P, E, FB, P], F32R)
        w2_lo = sb("w2_lo", [P, E, FB, P], F32R)
        wr_sb = sb("wr_sb", [P, E])
        ffn_split = sem("ffn_split")
        ident_ready = sem("ident_ready")

        attention(nc, sb, sem, x, w_in, w_out, b_in, b_v, cols, alpha, alpha_row, w1, w2, w_router,
                  x_all, u_all, stats, mv, std, rstd, eps_col, ident, ident_ready,
                  (w1_hi, w1_lo, w2_hi, w2_lo), wr_sb, ffn_split, NT, G, TG, NB)
        experts(nc, sb, sem, out, x_all, u_all, stats, mv, std, rstd, eps_col, ident,
                (w1_hi, w1_lo, w2_hi, w2_lo), wr_sb, NT, G, TG)


def attention(nc, sb_, sem_, x, w_in, w_out, b_in, b_v, cols, alpha, alpha_row, w1, w2, w_router,
              x_all, u_all, stats, mv, std, rstd, eps_col, ident, ident_ready, ffn_w, wr_sb,
              ffn_split, NT, G, TG, NB):
    ctx = ExitStack()
    with ctx:
        def sb(name, shape, dt=F32):
            return sb_(name, shape, dt, ctx)

        def sem(name):
            return sem_(name, ctx)

        wi_hi = sb("wi_hi", [P, 4, CH], F32R)
        wi_lo = sb("wi_lo", [P, 4, CH], F32R)
        wo_hi = sb("wo_hi", [P, PAIRS, D], F32R)
        wo_lo = sb("wo_lo", [P, PAIRS, D], F32R)
        STG, CHUNK = 2, 512
        stage = sb("stage", [P, STG, CHUNK])
        bi = sb("bi", [P, 3, PAIRS])
        bv = sb("bv", [P, CH])
        col = sb("col", [P, 3])
        al = sb("al", [P, PAIRS])
        al_min = sb("al_min", [1, 1])
        narrow = sb("narrow", [1, 1], I32)
        pow_up = sb("pow_up", [P, PAIRS, 129])
        pow_dn = sb("pow_dn", [P, PAIRS, 129])
        mid_q = sb("mid_q", [P, PAIRS, 32])
        mid_k = sb("mid_k", [P, PAIRS, 32])
        mask = sb("mask", [P, 1 + len(LEVELS), 3, P], I8)
        xn = sb("xn", [P, GT])
        xn_hi = sb("xn_hi", [P, GT], F32R)
        xn_lo = sb("xn_lo", [P, GT], F32R)
        v_sb = sb("v_sb", [P, TG, CH])
        q_raw = sb("q_raw", [P, GT])
        k_raw = sb("k_raw", [P, GT])
        gate = sb("gate", [P, 2, GT])
        qv = sb("qv", [P, 2, NB, VER])
        kv = sb("kv", [P, 2, NB, VER])
        a_sb = sb("a_sb", [P, NB, 2, 3 * P])
        og = sb("og", [P, GT])
        z = og[:].rearrange("p (t d) -> p t d", t=TG)
        og_hi = sb("og_hi", [P, GT], F32R)
        og_lo = sb("og_lo", [P, GT], F32R)
        y_sb = sb("y_sb", [P, GT])

        al_row = v_sb[0:1, 0, :]
        it = q_raw[:, 0:2 * P].bitcast(I32).rearrange("p (a q) -> p a q", a=2)
        ring = ctx.enter_context(nc.psum_tensor("ring", [P, 2, 512], F32))
        sc = ctx.enter_context(nc.psum_tensor("sc", [P, NB, 2, 512], F32))
        ps_o = ctx.enter_context(nc.psum_tensor("ps_o", [P, 512], F32))
        ps_y = ctx.enter_context(nc.psum_tensor("ps_y", [P, 512], F32))

        x_in = [sem(f"x_in{g}") for g in range(G)]
        small_in = sem("small_in")
        stage_in = [sem(f"stage_in{i}") for i in range(STG)]
        hi_done = sem("hi_done")
        lo_done = sem("lo_done")
        stats_done = sem("stats_done")
        std_done = sem("std_done")
        sig_done = sem("sig_done")
        dve_step = sem("dve_step")
        mask_ready = sem("mask_ready")
        narrow_ready = sem("narrow_ready")
        z_ready = sem("z_ready")
        xn_raw = sem("xn_raw")
        xn_ready = sem("xn_ready")
        v_ready = sem("v_ready")
        ring_full = [sem(f"ring_full{r}") for r in range(2)]
        raw_ready = sem("raw_ready")
        ver_ready = sem("ver_ready")
        gate_ready = sem("gate_ready")
        sc_done = sem("sc_done")
        keep_turn = sem("keep_turn")
        a_ready = sem("a_ready")
        out_done = sem("out_done")
        o_read = sem("o_read")
        og_raw = sem("og_raw")
        og_ready = sem("og_ready")
        wo_done = sem("wo_done")
        y_ready = sem("y_ready")
        lv_ready = sem("lv_ready")
        xn_step = sem("xn_step")
        iota_ready = sem("iota_ready")
        x1_done = sem("x1_done")

        wi_h, wi_l = [w[:].rearrange("p a c -> p (a c)") for w in (wi_hi, wi_lo)]
        wo_h, wo_l = [w[:].rearrange("p a c -> p (a c)") for w in (wo_hi, wo_lo)]
        f_h = [w[:].rearrange("p e b c -> p (e b c)") for w in (ffn_w[0], ffn_w[2])]
        f_l = [w[:].rearrange("p e b c -> p (e b c)") for w in (ffn_w[1], ffn_w[3])]
        chunks = [(w_in, wi_h, wi_l, c) for c in range(0, 4 * CH, CHUNK)]
        chunks += [(w_out, wo_h, wo_l, c) for c in range(0, CH, CHUNK)]
        FIRST = len(chunks)
        for i, src in enumerate((w1, w2)):
            chunks += [(src, f_h[i], f_l[i], c * CHUNK) for c in range(E * DFF // CHUNK)]

        GROUPS = 1 + 2 * TG + 3 * PAIRS + 1
        assert GROUPS % 2 == 0

        def slot(i):
            return i % 2, i // 2

        def proj_use(p, j):
            return 1 + 2 * TG + 3 * p + j

        def read_by(i, g):
            if i == 0:
                return xn_raw, g + 1
            if i <= 2 * TG:
                return v_ready, 2 * TG * g + i
            p, j = divmod(i - 1 - 2 * TG, 3)
            return (raw_ready, 2 * (PAIRS * g + p) + j + 1) if j < 2 else (gate_ready, PAIRS * g + p + 1)

        block = ctx.enter_context(nc.Block())

        @block.sync
        def _(sp):
            xv = x.rearrange("(t p) d -> p t d", p=P)
            for g in range(G):
                sp.dma_start(x_all[:, g * TG:(g + 1) * TG, :], xv[:, g * TG:(g + 1) * TG, :])\
                  .then_inc(x_in[g], 16)
            for n, (src, _, _, c) in enumerate(chunks):
                if n >= STG:
                    sp.wait_ge(lo_done, n - STG + 1)
                sp.dma_start(stage[:, n % STG, :], src[:, c:c + CHUNK]).then_inc(stage_in[n % STG], 16)

        @block.gpsimd
        def _(pool):
            nc.gpsimd.memset(ident[:], 1.0).then_inc(mask_ready, 1)
            causal = k_raw[:, 0:3 * P].rearrange("p (t q) -> p t q", t=3)
            nc.gpsimd.memset(causal, 1.0).then_inc(mask_ready, 1)
            pool.wait_ge(mask_ready, 2)
            nc.gpsimd.affine_select(out=ident[:], in_=ident[:], compare_op=ALU.is_equal, fill=0.0, base=0,
                                    pattern=[[1, P]], channel_multiplier=-1).then_inc(ident_ready, 1)
            for t in (0, 2):
                nc.gpsimd.affine_select(out=causal[:, t, :], in_=causal[:, t, :], compare_op=ALU.is_ge, fill=0.0,
                                        base=0, pattern=[[1, P]], channel_multiplier=-1).then_inc(mask_ready, 1)
            nc.gpsimd.iota(it[:, 0, :], pattern=[[1, P]], base=0, channel_multiplier=0).then_inc(iota_ready, 1)
            nc.gpsimd.iota(it[:, 1, :], pattern=[[0, P]], base=0, channel_multiplier=1).then_inc(iota_ready, 1)
            for n, (_, hi, lo, c) in enumerate(chunks):
                st, h, l = stage[:, n % STG, :], hi[:, c:c + CHUNK], lo[:, c:c + CHUNK]
                if n < FIRST:
                    pool.wait_ge(hi_done, n + 1)
                else:
                    pool.wait_ge(stage_in[n % STG], 16 * (n // STG + 1))
                    nc.gpsimd.tensor_copy(h, st).then_inc(ffn_split, 1)
                    pool.wait_ge(ffn_split, n - FIRST + 1)
                nc.gpsimd.tensor_tensor(l, st, h.bitcast(F32), ALU.subtract).then_inc(lo_done, 1)

        @block.scalar
        def _(act):
            act.dma_start(bi[:], b_in).then_inc(small_in, 16)
            act.dma_start(bv[:], b_v.to_broadcast([P, CH])).then_inc(small_in, 16)
            act.dma_start(col[:], cols).then_inc(small_in, 16)
            act.dma_start(al[:], alpha).then_inc(small_in, 16)
            act.dma_start(al_row, alpha_row).then_inc(small_in, 16)
            act.dma_start(wr_sb[:], w_router).then_inc(small_in, 16)
            act.wait_ge(small_in, 96)
            nc.scalar.activation(pow_up[:, :, 1], al[:], ACT.Sigmoid).then_inc(sig_done, 1)
            for n in range(FIRST):
                _, hi, _, c = chunks[n]
                act.wait_ge(stage_in[n % STG], 16 * (n // STG + 1))
                nc.scalar.activation(hi[:, c:c + CHUNK], stage[:, n % STG, :], ACT.Copy).then_inc(hi_done, 1)
                if n in (1, 3):
                    act.wait_ge(stats_done, n // 2 + 1)
                    nc.scalar.activation(std[:], mv[:, :, 1], ACT.Sqrt, bias=eps_col[:, 0:1])\
                      .then_inc(std_done, 1)

            def body():
                with act.Fori(0, G) as g:
                    def full(i):
                        bank, n = slot(i)
                        act.wait_ge(ring_full[bank], g * (GROUPS // 2) + n + 1)
                        return ring[:, bank, :]

                    src = full(0)
                    nc.scalar.activation(xn[:], src, ACT.Identity, bias=col[:, 2:3],
                                         scale=col[:, 1:2]).then_inc(xn_raw, 1)

                    def evac(p):
                        for j, dst in enumerate((q_raw, k_raw)):
                            src = full(proj_use(p, j))
                            act.wait_ge(ver_ready, 2 * (PAIRS * g + p) + j + 1)
                            nc.scalar.activation(dst[:], src, ACT.Identity, bias=bi[:, j, p:p + 1])\
                              .then_inc(raw_ready, 1)
                        src = full(proj_use(p, 2))
                        act.wait_ge(og_ready, PAIRS * g + p + 1)
                        nc.scalar.activation(gate[:, p % 2, :], src, ACT.Silu, bias=bi[:, 2, p:p + 1])\
                          .then_inc(gate_ready, 1)

                    for p in range(PAIRS):
                        evac(p)
                    act.wait_ge(wo_done, 1 + PAIRS * g + PAIRS)
                    nc.scalar.activation(y_sb[:], ps_y[:], ACT.Identity, bias=col[:, 0:1]).then_inc(y_ready, 1)

            body()

        @block.tensor
        def _(pe):
            def body(levels):
                R = 1 + len(levels)
                pe.sem_inc(sc_done, 2 * R + 1)
                with pe.Fori(0, G) as g:
                    def claim(i):
                        bank, _ = slot(i)
                        if i >= 2:
                            pe.wait_ge(*read_by(i - 2, g))
                        return ring[:, bank, :], ring_full[bank]

                    def three(dst, w_hi, w_lo, x_hi, x_lo, start=True, stop=True):
                        nc.tensor.matmul(dst, w_hi, x_hi, start=start, stop=False)
                        nc.tensor.matmul(dst, w_hi, x_lo, start=False, stop=False)
                        return nc.tensor.matmul(dst, w_lo, x_hi, start=False, stop=stop)

                    dst, full = claim(0)
                    pe.wait_ge(z_ready, g + 1)
                    for t in range(TG):
                        mm = nc.tensor.transpose(dst[:, t * P:(t + 1) * P], z[:, t, :], ident[:])
                    mm.then_inc(full, 1)
                    pe.wait_ge(xn_ready, g + 1)
                    for t in range(TG):
                        rows = slice(t * P, (t + 1) * P)
                        for h in range(2):
                            dst, full = claim(1 + 2 * t + h)
                            c = slice(h * 512, (h + 1) * 512)
                            three(dst, xn_hi[:, rows], xn_lo[:, rows], wi_hi[:, 3, c], wi_lo[:, 3, c])\
                                .then_inc(full, 1)

                    def proj(p):
                        c = slice(p * P, (p + 1) * P)
                        for j in range(3):
                            dst, full = claim(proj_use(p, j))
                            three(dst, wi_hi[:, j, c], wi_lo[:, j, c], xn_hi[:], xn_lo[:]).then_inc(full, 1)

                    def diagonal(p, b, r, c0):
                        h = slice(r * DH, (r + 1) * DH)
                        for t in range(2):
                            mm = nc.tensor.matmul(sc[:, b, r, 2 * t * P:2 * t * P + P],
                                                  kv[h, p % 2, b, c0 + t * P:c0 + (t + 1) * P],
                                                  qv[h, p % 2, b, c0 + t * P:c0 + (t + 1) * P],
                                                  start=True, stop=True)
                        return mm

                    def scores(p):
                        n = PAIRS * g + p
                        pe.wait_ge(ver_ready, 2 + 2 * n + 2)
                        for b in range(NB):
                            pe.wait_ge(a_ready, 2 * R * n + b + 1)
                            for r in range(2):
                                diagonal(p, b, r, MID)
                            for r in range(2):
                                h = slice(r * DH, (r + 1) * DH)
                                for t in range(2):
                                    for L, c in ((32, S32), (64, S64)):
                                        for i in range(64 // L):
                                            s0 = c + 64 * t + i * L
                                            key = 2 * L * i
                                            q0 = 2 * t * P + key + L
                                            nc.tensor.matmul(sc[key:key + L, b, r, q0:q0 + L],
                                                             kv[h, p % 2, b, s0:s0 + L],
                                                             qv[h, p % 2, b, s0:s0 + L],
                                                             start=True, stop=True)
                                mm = nc.tensor.matmul(sc[:, b, r, P:2 * P], kv[h, p % 2, b, S128:S128 + P],
                                                      qv[h, p % 2, b, S128:S128 + P], start=True, stop=True)
                            mm.then_inc(sc_done, 1)
                        for i, L in enumerate(levels):
                            pe.wait_ge(lv_ready, len(levels) * n + i + 1)
                            for b in range(NB):
                                pe.wait_ge(a_ready, 2 * R * n + 2 * (i + 1) + b + 1)
                                for r in range(2):
                                    mm = diagonal(p, b, r, S32)
                                mm.then_inc(sc_done, 1)

                    def outs(p):
                        n = PAIRS * g + p
                        if p == 0:
                            pe.wait_ge(v_ready, 2 * TG * (g + 1))
                        pe.wait_ge(o_read, n + 1)
                        for b in range(NB):
                            pe.wait_ge(a_ready, 2 + 2 * R * n + 2 * (R - 1) + b + 1)
                            dst = ps_o[:, b * SEQ:(b + 1) * SEQ]
                            c = [slice(p * P + r * DH, p * P + (r + 1) * DH) for r in range(2)]
                            for r in range(2):
                                nc.tensor.matmul(dst[r * DH:(r + 1) * DH, :], v_sb[:, 2 * b, c[r]],
                                                 a_sb[:, b, r, 0:2 * P], start=True, stop=False,
                                                 skip_group_check=True)
                            for r in range(2):
                                mm = nc.tensor.matmul(dst[r * DH:(r + 1) * DH, P:2 * P],
                                                      v_sb[:, 2 * b + 1, c[r]], a_sb[:, b, r, 2 * P:3 * P],
                                                      start=False, stop=True, skip_group_check=True)
                            mm.then_inc(out_done, 1)

                    def project_out(p):
                        n = PAIRS * g + p
                        pe.wait_ge(og_ready, 2 + n + 1)
                        three(ps_y[:], wo_hi[:, p, :], wo_lo[:, p, :], og_hi[:], og_lo[:], start=(p == 0),
                              stop=(p == PAIRS - 1)).then_inc(wo_done, 1)

                    proj(0)
                    for p in range(PAIRS):
                        if p + 1 < PAIRS:
                            proj(p + 1)
                        scores(p)
                        if p:
                            project_out(p - 1)
                        outs(p)
                    project_out(PAIRS - 1)
                    dst, full = claim(GROUPS - 1)
                    pe.wait_ge(y_ready, g + 1)
                    for t in range(TG):
                        mm = nc.tensor.transpose(dst[:, t * P:(t + 1) * P], y_sb[:, t * P:(t + 1) * P],
                                                 ident[:])
                    mm.then_inc(full, 1)

            pe.wait_ge(ident_ready, 1)
            pe.wait_ge(lo_done, FIRST)
            pe.sem_inc(out_done, 2)
            pe.sem_inc(wo_done, 1)
            pe.wait_ge(narrow_ready, 1)
            small_logit = pe.value_load(narrow[0:1, 0:1], min_val=0, max_val=1)
            with pe.If(small_logit):
                body(LEVELS)
            with pe.Else():
                body([])

        @block.vector
        def _(dve):
            step = [0]

            def chain(ins):
                step[0] += 1
                ins.then_inc(dve_step, 1)
                dve.wait_ge(dve_step, step[0])

            def tile_stats(src, tiles):
                for t in tiles:
                    last = nc.vector.bn_stats(stats[:, t, :], src[:, t, :])
                chain(last)
                for t in tiles:
                    last = nc.vector.bn_aggr(mv[:, t, :], stats[:, t, :])
                return last

            nc.vector.memset(eps_col[:], EPS)
            nc.vector.memset(a_sb[:], 0.0)
            nc.vector.memset(pow_up[:, :, 0], 1.0)
            chain(nc.vector.memset(pow_dn[:, :, 128], 1.0))
            for g in range(G):
                dve.wait_ge(x_in[g], 16)
                last = tile_stats(x_all, range(g * TG, (g + 1) * TG))
            last.then_inc(stats_done, 1)
            dve.wait_ge(small_in, 96)
            chain(nc.vector.tensor_reduce(al_min[:], al_row, AX.X, ALU.min))
            nc.vector.tensor_scalar(narrow[:], al_min[:], LOGIT_MIN, None, ALU.is_lt).then_inc(narrow_ready, 1)
            dve.wait_ge(sig_done, 1)
            chain(nc.vector.tensor_copy(pow_dn[:, :, 127], pow_up[:, :, 1]))
            k = 1
            while k < 128:
                a_k = pow_up[:, :, k:k + 1].to_broadcast([P, PAIRS, k])
                nc.vector.tensor_tensor(pow_up[:, :, k + 1:2 * k + 1], pow_up[:, :, 1:k + 1], a_k, ALU.mult)
                chain(nc.vector.tensor_tensor(pow_dn[:, :, 128 - 2 * k:128 - k], pow_dn[:, :, 128 - k:128],
                                              a_k, ALU.mult))
                k *= 2
            nc.vector.reciprocal(mid_q[:, :, 0:16], pow_dn[:, :, 112:128])
            nc.vector.tensor_copy(mid_q[:, :, 16:32], pow_up[:, :, 0:16])
            nc.vector.tensor_copy(mid_k[:, :, 0:16], pow_dn[:, :, 112:128])
            nc.vector.reciprocal(mid_k[:, :, 16:32], pow_up[:, :, 0:16])
            dve.wait_ge(std_done, 1)
            chain(nc.vector.reciprocal(rstd[:], std[:]))
            for t in range(NT):
                last = nc.vector.tensor_scalar(u_all[:, t, :], x_all[:, t, :], mv[:, t, 0:1], rstd[:, t:t + 1],
                                               ALU.subtract, ALU.mult)
            chain(last)
            tile_stats(u_all, range(NT)).then_inc(stats_done, 1)
            chain(nc.vector.tensor_tensor(x_all[:], x_all[:], u_all[:], ALU.add))
            dve.wait_ge(std_done, 2)
            chain(nc.vector.reciprocal(rstd[:], std[:]))
            dve.sem_inc(ver_ready, 2)
            dve.sem_inc(a_ready, 2)
            dve.sem_inc(o_read, 1)
            dve.sem_inc(og_ready, 2)
            dve.wait_ge(mask_ready, 4)

            def body(levels):
                R = 1 + len(levels)
                with dve.Fori(0, G) as g:
                    def full(i):
                        bank, n = slot(i)
                        dve.wait_ge(ring_full[bank], g * (GROUPS // 2) + n + 1)
                        return ring[:, bank, :]

                    for t in range(TG):
                        tt = bass.ds(g * TG + t, 1)
                        last = nc.vector.tensor_scalar(z[:, t, :], u_all[:, tt, :], mv[:, tt, 0],
                                                       rstd[:, tt], ALU.subtract, ALU.mult)
                    last.then_inc(z_ready, 1)
                    dve.wait_ge(xn_raw, g + 1)
                    nc.vector.tensor_copy(xn_hi[:], xn[:]).then_inc(xn_step, 1)
                    dve.wait_ge(xn_step, g + 1)
                    nc.vector.tensor_tensor(xn_lo[:], xn[:], xn_hi[:].bitcast(F32), ALU.subtract)\
                      .then_inc(xn_ready, 1)
                    for t in range(TG):
                        for h in range(2):
                            src = full(1 + 2 * t + h)
                            c = slice(h * 512, (h + 1) * 512)
                            nc.vector.tensor_tensor(v_sb[:, t, c], src, bv[:, c], ALU.add).then_inc(v_ready, 1)

                    def decayed(dst, raw, p, odd, tab_mid, tab):
                        def spans(L):
                            return raw[:].rearrange("c (b n o l) -> c b n o l", b=NB, o=2, l=L)[:, :, :, odd, :]

                        if R == 1:
                            nc.vector.tensor_tensor(
                                dst[:, p % 2, :, MID:S32].rearrange("c b (n l) -> c b n l", l=32),
                                raw[:].rearrange("c (b n l) -> c b n l", b=NB, l=32),
                                tab_mid[:, p:p + 1, :].unsqueeze(1).to_broadcast([P, NB, SEQ // 32, 32]),
                                ALU.mult)
                        else:
                            nc.vector.tensor_copy(dst[:, p % 2, :, MID:S32],
                                                  raw[:].rearrange("c (b n) -> c b n", b=NB))
                        for L, c in ((32, S32), (64, S64), (128, S128)):
                            n = SEQ // (2 * L)
                            last = nc.vector.tensor_tensor(
                                dst[:, p % 2, :, c:c + P].rearrange("c b (n l) -> c b n l", l=L), spans(L),
                                tab(p, L).unsqueeze(1).to_broadcast([P, NB, n, L]), ALU.mult)
                        return last

                    def up(p, L):
                        return pow_up[:, p:p + 1, 0:L]

                    def down(p, L):
                        return pow_dn[:, p:p + 1, P - L:P]

                    def versions(p):
                        n = PAIRS * g + p
                        dve.wait_ge(sc_done, 2 * R * n + 1)
                        dve.wait_ge(raw_ready, 2 * n + 1)
                        decayed(qv, q_raw, p, 1, mid_q, up).then_inc(ver_ready, 1)
                        dve.wait_ge(raw_ready, 2 * n + 2)
                        decayed(kv, k_raw, p, 0, mid_k, down).then_inc(ver_ready, 1)

                    def keep(b, i):
                        m = mask[:, i, :, :].rearrange("p t q -> p (t q)").unsqueeze(1)
                        dve.sem_inc(keep_turn, 1)
                        nc.vector.copy_predicated(a_sb[:, b, :, :], m.to_broadcast([P, 2, 3 * P]),
                                                  sc[:, b, :, 0:3 * P]).then_inc(a_ready, 1)

                    def level(dst, p, tab, L):
                        return nc.vector.tensor_tensor(
                            dst[:, p % 2, :, S32:S32 + SEQ].rearrange("c b (n l) -> c b n l", l=L),
                            dst[:, p % 2, :, MID:MID + SEQ].rearrange("c b (n l) -> c b n l", l=L),
                            tab(p, L).unsqueeze(1).to_broadcast([P, NB, SEQ // L, L]), ALU.mult)

                    def masked(p):
                        n = PAIRS * g + p
                        for b in range(NB):
                            dve.wait_ge(sc_done, 2 * R + 1 + 2 * R * n + b + 1)
                            dve.wait_ge(out_done, 2 * n + b + 1)
                            keep(b, 0)
                        for i, L in enumerate(levels):
                            level(qv, p, up, L)
                            level(kv, p, down, L).then_inc(lv_ready, 1)
                            for b in range(NB):
                                dve.wait_ge(sc_done, 2 * R + 1 + 2 * R * n + 2 * (i + 1) + b + 1)
                                keep(b, 1 + i)

                    def gated(p):
                        n = PAIRS * g + p
                        dve.wait_ge(out_done, 2 + 2 * n + 2)
                        dve.wait_ge(gate_ready, n + 1)
                        nc.vector.tensor_tensor(og[:], ps_o[:], gate[:, p % 2, :], ALU.mult).then_inc(o_read, 1)
                        dve.wait_ge(o_read, 1 + n + 1)
                        dve.wait_ge(wo_done, n + 1)
                        nc.vector.tensor_copy(og_hi[:], og[:]).then_inc(og_raw, 1)
                        dve.wait_ge(og_raw, n + 1)
                        nc.vector.tensor_tensor(og_lo[:], og[:], og_hi[:].bitcast(F32), ALU.subtract)\
                          .then_inc(og_ready, 1)

                    versions(0)
                    for p in range(PAIRS):
                        if p + 1 < PAIRS:
                            versions(p + 1)
                        masked(p)
                        gated(p)
                    src = full(GROUPS - 1)
                    rows = bass.ds(g * TG, TG)
                    nc.vector.tensor_tensor(x_all[:, rows, :], src.rearrange("p (t d) -> p t d", t=TG),
                                            x_all[:, rows, :], ALU.add).then_inc(x1_done, 1)

            causal = k_raw[:, 0:3 * P].rearrange("p (t q) -> p t q", t=3)

            def general_masks():
                nc.vector.tensor_copy(mask[:, 0, :, :], causal)
                nc.vector.memset(mask[:, 1:, 1, :], 0)
                dve.wait_ge(iota_ready, 2)
                apart, test = xn[:, 0:P], xn[:, P:2 * P]
                xor = xn[:, 2 * P:3 * P].bitcast(I32)
                chain(nc.vector.tensor_tensor(xor, it[:, 0, :], it[:, 1, :], ALU.bitwise_xor))
                chain(nc.vector.tensor_copy(apart, xor))
                for i, L in enumerate(LEVELS):
                    chain(nc.vector.tensor_scalar(test, apart, float(L), None, ALU.is_ge))
                    chain(nc.vector.scalar_tensor_tensor(out=test, in0=apart, scalar=float(2 * L), in1=test,
                                                         op0=ALU.is_lt, op1=ALU.mult))
                    for t in (0, 2):
                        nc.vector.tensor_tensor(mask[:, 1 + i, t, :], test, causal[:, t, :], ALU.mult)
                chain(nc.vector.tensor_scalar(test, apart, 32.0, None, ALU.is_ge))
                chain(nc.vector.scalar_tensor_tensor(out=test, in0=apart, scalar=0.0, in1=test,
                                                     op0=ALU.is_equal, op1=ALU.add))
                for t in (0, 2):
                    last = nc.vector.tensor_tensor(mask[:, 0, t, :], test, causal[:, t, :], ALU.mult)
                chain(last)
            small_logit = dve.value_load(narrow[0:1, 0:1], min_val=0, max_val=1)
            with dve.If(small_logit):
                general_masks()
                body(LEVELS)
            with dve.Else():
                nc.vector.tensor_copy(mask[:, 0, :, :], causal)
                body([])


def experts(nc, sb_, sem_, out, x_all, u_all, stats, mv, std, rstd, eps_col, ident, ffn_w, wr_sb,
            NT, G, TG):
    T = NT * P
    HR = 4
    K = E * FB
    ctx = ExitStack()
    with ctx:
        def sb(name, shape, dt=F32):
            return sb_(name, shape, dt, ctx)

        def sem(name):
            return sem_(name, ctx)

        xt = sb("xt", [P, T])
        xt_hi = sb("xt_hi", [P, T], F32R)
        xt_lo = sb("xt_lo", [P, T], F32R)
        lg = sb("lg", [P, NT, E])
        ex = sb("ex", [P, NT, E])
        cand = sb("cand", [P, NT, E])
        first = sb("first", [P, NT, E])
        second = sb("second", [P, NT, E])
        rest = sb("rest", [P, NT, E])
        red = sb("red", [P, NT])
        rank = sb("rank", [P, E])
        gates = sb("gates", [P, NT, 64], F32R)
        gates_t = sb("gates_t", [64, T], F32R)
        pick_f = sb("pick_f", [64, E, P])
        pick = sb("pick", [64, E, P], F32R)
        h = sb("h", [P, 2, GT])
        h_hi = sb("h_hi", [P, HR, GT], F32R)
        h_lo = sb("h_lo", [P, HR, GT], F32R)
        gb = sb("gb", [P, 2, GT])
        part = sb("part", [P, GT])
        acc = sb("acc", [P, GT])
        ps = ctx.enter_context(nc.psum_tensor("ps", [P, 8, 512], F32))
        Y, GB, TR = 4, 6, 7

        stats2 = sem("stats2")
        std2 = sem("std2")
        u_ready = sem("u_ready")
        dve_step2 = sem("dve_step2")
        turned = sem("turned")
        xt_ready = sem("xt_ready")
        xt_split = sem("xt_split")
        logits_done = sem("logits_done")
        centred = sem("centred")
        exp_done = sem("exp_done")
        rank_ready = sem("rank_ready")
        pick_ready = sem("pick_ready")
        pick_split = sem("pick_split")
        gates_ready = sem("gates_ready")
        gates_turned = sem("gates_turned")
        gates_t_ready = sem("gates_t_ready")
        h_full = sem("h_full")
        h_act = sem("h_act")
        h_hi_done = sem("h_hi_done")
        h_split = sem("h_split")
        y_step = sem("y_step")
        gb_full = sem("gb_full")
        gb_turn = sem("gb_turn")
        gb_ready = sem("gb_ready")
        y_used = sem("y_used")
        acc_step = sem("acc_step")
        acc_turned = sem("acc_turned")
        out_ready = sem("out_ready")
        out_sent = sem("out_sent")
        block = ctx.enter_context(nc.Block())

        @block.sync
        def _(sp):
            ov = out.rearrange("(t p) d -> p t d", p=P)
            for g in range(G):
                sp.wait_ge(out_ready, g + 1)
                sp.dma_start(ov[:, g * TG:(g + 1) * TG, :], x_all[:, g * TG:(g + 1) * TG, :]).then_inc(out_sent, 16)
            sp.wait_ge(out_sent, 16 * G)

        @block.gpsimd
        def _(pool):
            for e in range(E):
                last = nc.gpsimd.memset(rank[:, e:e + 1], float(E - e))
            last.then_inc(rank_ready, 1)
            nc.gpsimd.memset(pick_f[:], 1.0).then_inc(pick_ready, 1)
            pool.wait_ge(pick_ready, 1)
            for k in range(2):
                rows = slice(32 * k, 32 * k + 32)
                nc.gpsimd.affine_select(out=pick_f[rows, :, :], in_=pick_f[rows, :, :], compare_op=ALU.is_equal,
                                        fill=0.0, base=0, pattern=[[-1, E], [0, P]],
                                        channel_multiplier=1).then_inc(pick_ready, 1)

        @block.scalar
        def _(act):
            act.wait_ge(stats2, 1)
            nc.scalar.activation(std[:], mv[:, :, 1], ACT.Sqrt, bias=eps_col[:, 0:1]).then_inc(std2, 1)
            for g in range(G):
                act.wait_ge(turned, g + 1)
                nc.scalar.activation(xt[:, g * GT:(g + 1) * GT], ps[:, g, :], ACT.Copy).then_inc(xt_ready, 1)
            act.wait_ge(centred, 1)
            nc.scalar.activation(ex[:], lg[:], ACT.Exp).then_inc(exp_done, 1)
            for g in range(G):
                act.wait_ge(gates_turned, g + 1)
                nc.scalar.activation(gates_t[:, g * GT:(g + 1) * GT], ps[0:64, g, :], ACT.Copy)\
                  .then_inc(gates_t_ready, 1)
            act.sem_inc(gb_ready, 1)
            with act.Fori(0, G) as g:
                for k in range(K):
                    n = K * g + k
                    act.wait_ge(h_full, n + 1)
                    act.wait_ge(h_split, n + 1)
                    nc.scalar.activation(h[:, k % 2, :], ps[:, k % HR, :], ACT.Silu).then_inc(h_act, 1)
                    if k % FB == FB - 1:
                        e = k // FB
                        act.wait_ge(gb_full, E * g + e + 1)
                        act.wait_ge(y_used, E * g + e + 1)
                        nc.scalar.activation(gb[:, e % 2, :], ps[:, GB, :], ACT.Copy).then_inc(gb_ready, 1)

        @block.tensor
        def _(pe):
            def three(dst, w_hi, w_lo, x_hi, x_lo, start=True, stop=True):
                nc.tensor.matmul(dst, w_hi, x_hi, start=start, stop=False)
                nc.tensor.matmul(dst, w_hi, x_lo, start=False, stop=False)
                return nc.tensor.matmul(dst, w_lo, x_hi, start=False, stop=stop)

            for g in range(G):
                pe.wait_ge(u_ready, g + 1)
                for t in range(TG):
                    mm = nc.tensor.transpose(ps[:, g, t * P:(t + 1) * P], u_all[:, g * TG + t, :], ident[:])
                mm.then_inc(turned, 1)
            for g in range(G):
                pe.wait_ge(xt_ready, g + 1)
                for t in range(g * TG, (g + 1) * TG):
                    mm = nc.tensor.matmul(ps[:, TR, t * E:(t + 1) * E], xt[:, t * P:(t + 1) * P], wr_sb[:],
                                          start=True, stop=True)
            mm.then_inc(logits_done, 1)
            pe.wait_ge(gates_ready, 1)
            for g in range(G):
                for t in range(TG):
                    mm = nc.tensor.transpose(ps[0:64, g, t * P:(t + 1) * P],
                                             gates[:, g * TG + t, :].bitcast(F32), ident[:])
                mm.then_inc(gates_turned, 1)
            pe.wait_ge(gates_t_ready, G)
            pe.wait_ge(xt_split, G)
            pe.wait_ge(pick_split, 1)
            pe.sem_inc(y_step, HR)
            with pe.Fori(0, G) as g:
                cols = bass.ds(g * GT, GT)

                def hidden(k):
                    e, f = divmod(k, FB)
                    three(ps[:, k % HR, :], ffn_w[0][:, e, f, :], ffn_w[1][:, e, f, :], xt_hi[:, cols],
                          xt_lo[:, cols]).then_inc(h_full, 1)
                    if f == 1:
                        pe.wait_ge(gb_ready, E * g + e + 1)
                        pe.sem_inc(gb_turn, 1)
                        nc.tensor.matmul(ps[:, GB, :], pick[:, e, :], gates_t[:, cols], start=True, stop=True)\
                          .then_inc(gb_full, 1)

                def back(k):
                    e, f = divmod(k, FB)
                    if f == 0:
                        pe.wait_ge(y_used, E * g + e + 1)
                    pe.wait_ge(h_split, 2 + K * g + k + 1)
                    three(ps[:, Y + e % 2, :], ffn_w[2][:, e, f, :], ffn_w[3][:, e, f, :], h_hi[:, k % HR, :],
                          h_lo[:, k % HR, :], start=(f == 0), stop=(f == FB - 1)).then_inc(y_step, 1)

                LAG = 2
                for k in range(K + LAG):
                    if k < K:
                        hidden(k)
                    if k >= LAG:
                        back(k - LAG)
                pe.wait_ge(acc_step, E * (g + 1))
                for t in range(TG):
                    mm = nc.tensor.transpose(ps[:, TR, t * P:(t + 1) * P], acc[:, t * P:(t + 1) * P], ident[:])
                mm.then_inc(acc_turned, 1)

        @block.vector
        def _(dve):
            step = [0]

            def chain(ins):
                step[0] += 1
                ins.then_inc(dve_step2, 1)
                dve.wait_ge(dve_step2, step[0])

            for t in range(NT):
                last = nc.vector.bn_stats(stats[:, t, :], x_all[:, t, :])
            chain(last)
            for t in range(NT):
                last = nc.vector.bn_aggr(mv[:, t, :], stats[:, t, :])
            last.then_inc(stats2, 1)
            dve.wait_ge(rank_ready, 1)
            nc.vector.memset(gates[:].bitcast(F32), 0.0)
            dve.wait_ge(pick_ready, 3)
            nc.vector.tensor_copy(pick[:], pick_f[:]).then_inc(pick_split, 1)
            dve.wait_ge(std2, 1)
            chain(nc.vector.reciprocal(rstd[:], std[:]))
            for t in range(NT):
                ins = nc.vector.tensor_scalar(u_all[:, t, :], x_all[:, t, :], mv[:, t, 0:1], rstd[:, t:t + 1],
                                              ALU.subtract, ALU.mult)
                if t % TG == TG - 1:
                    ins.then_inc(u_ready, 1)
            for g in range(G):
                cols = slice(g * GT, (g + 1) * GT)
                dve.wait_ge(xt_ready, g + 1)
                chain(nc.vector.tensor_copy(xt_hi[:, cols], xt[:, cols]))
                nc.vector.tensor_tensor(xt_lo[:, cols], xt[:, cols], xt_hi[:, cols].bitcast(F32), ALU.subtract)\
                  .then_inc(xt_split, 1)

            def wide(a):
                return a[:].unsqueeze(2).to_broadcast([P, NT, E])

            ranks = rank[:].unsqueeze(1).to_broadcast([P, NT, E])

            def largest(src, hot):
                chain(nc.vector.tensor_reduce(red[:], src, AX.X, ALU.max))
                chain(nc.vector.tensor_tensor(cand[:], src, wide(red), ALU.is_equal))
                chain(nc.vector.tensor_tensor(cand[:], cand[:], ranks, ALU.mult))
                chain(nc.vector.tensor_reduce(red[:], cand[:], AX.X, ALU.max))
                chain(nc.vector.tensor_tensor(hot[:], cand[:], wide(red), ALU.is_equal))

            dve.wait_ge(logits_done, 1)
            logits = ps[:, TR, 0:NT * E].rearrange("p (t e) -> p t e", e=E)
            chain(nc.vector.tensor_reduce(red[:], logits, AX.X, ALU.max))
            nc.vector.tensor_tensor(lg[:], logits, wide(red), ALU.subtract).then_inc(centred, 1)
            dve.wait_ge(centred, 1)
            largest(lg[:], first)
            chain(nc.vector.scalar_tensor_tensor(out=rest[:], in0=first[:], scalar=NEG, in1=lg[:], op0=ALU.mult,
                                                 op1=ALU.add))
            largest(rest[:], second)
            chain(nc.vector.tensor_tensor(first[:], first[:], second[:], ALU.add))
            dve.wait_ge(exp_done, 1)
            chain(nc.vector.tensor_tensor(first[:], first[:], ex[:], ALU.mult))
            chain(nc.vector.tensor_reduce(red[:], first[:], AX.X, ALU.add))
            chain(nc.vector.reciprocal(red[:], red[:]))
            chain(nc.vector.tensor_tensor(first[:], first[:], wide(red), ALU.mult))
            chain(nc.vector.tensor_copy(gates[:, :, 0:E], first[:]))
            nc.vector.tensor_tensor(gates[:, :, 32:32 + E], first[:], gates[:, :, 0:E].bitcast(F32),
                                    ALU.subtract).then_inc(gates_ready, 1)
            dve.sem_inc(h_split, 2)
            dve.sem_inc(y_used, 2)

            def gather(g, e):
                m = E * g + e
                dve.wait_ge(y_step, HR + FB * (m + 1))
                dve.wait_ge(gb_ready, 1 + m + 1)
                y = ps[:, Y + e % 2, :]
                if e == 0:
                    nc.vector.tensor_tensor(acc[:], y, gb[:, e % 2, :], ALU.mult).then_inc(y_used, 1)
                    dve.wait_ge(y_used, 2 + m + 1)
                    dve.sem_inc(acc_step, 1)
                else:
                    nc.vector.tensor_tensor(part[:], y, gb[:, e % 2, :], ALU.mult).then_inc(y_used, 1)
                    dve.wait_ge(y_used, 2 + m + 1)
                    nc.vector.tensor_tensor(acc[:], acc[:], part[:], ALU.add).then_inc(acc_step, 1)
                    dve.wait_ge(acc_step, m + 1)

            with dve.Fori(0, G) as g:
                for k in range(K):
                    n = K * g + k
                    dve.wait_ge(h_act, n + 1)
                    dve.wait_ge(y_step, n + 1)
                    nc.vector.tensor_copy(h_hi[:, k % HR, :], h[:, k % 2, :]).then_inc(h_hi_done, 1)
                    dve.wait_ge(h_hi_done, n + 1)
                    nc.vector.tensor_tensor(h_lo[:, k % HR, :], h[:, k % 2, :], h_hi[:, k % HR, :].bitcast(F32),
                                            ALU.subtract).then_inc(h_split, 1)
                    if k >= FB and k % FB == FB - 1:
                        gather(g, k // FB - 1)
                gather(g, E - 1)
                dve.wait_ge(acc_turned, g + 1)
                rows = bass.ds(g * TG, TG)
                nc.vector.tensor_tensor(x_all[:, rows, :], ps[:, TR, :].rearrange("p (t d) -> p t d", t=TG),
                                        x_all[:, rows, :], ALU.add).then_inc(out_ready, 1)


def kernel(**inputs):
    import numpy as np
    import concourse.bacc as bacc
    from concourse.bass_utils import run_bass_kernel_spmd

    a = {k.replace("L0_attn_", "").replace("L0_ffn_", ""): np.asarray(v) for k, v in inputs.items()}
    by_channel = lambda v: v.reshape(PAIRS, P).T
    arrays = {
        "x": a["x"].reshape(-1, D),
        "w_in": np.concatenate([a[n].T for n in ("WQ", "WK", "Wg", "WV")], axis=1),
        "w_out": a["WO"].T.reshape(PAIRS, P, D).transpose(1, 0, 2).reshape(P, CH),
        "b_in": np.stack([by_channel(a[n]) for n in ("bQ", "bK", "bg")], axis=1),
        "b_v": a["bV"].reshape(1, CH),
        "cols": np.stack([a["bO"], a["ln_gamma"], a["ln_beta"]], axis=1),
        "alpha": by_channel(a["alpha_logit"].reshape(-1)),
        "alpha_row": a["alpha_logit"].reshape(1, CH),
        "w1": a["W1"].transpose(2, 0, 1).reshape(D, E * DFF),
        "w2": a["W2"].reshape(E, D, FB, P).transpose(3, 0, 2, 1).reshape(P, E * DFF),
        "w_router": a["Wr"].T,
    }
    arrays = {f"in_{k}": np.ascontiguousarray(v) for k, v in arrays.items()}
    nc = bacc.Bacc("TRN2", target_bir_lowering=False, num_devices=1)
    args = [nc.dram_tensor(n, v.shape, mybir.dt.from_np(v.dtype), kind="ExternalInput").ap()
            for n, v in arrays.items()]
    out = nc.dram_tensor("out_0", arrays["in_x"].shape, F32, kind="ExternalOutput").ap()
    build(nc, *args, out)
    r = run_bass_kernel_spmd(nc, [arrays], core_ids=[0])
    return r.results[0]["out_0"].reshape(a["x"].shape)
```

```python
from contextlib import ExitStack

import concourse.bass as bass
from concourse import mybir

ALU = mybir.AluOpType
ACT = mybir.ActivationFunctionType
F32 = mybir.dt.float32
F32R = mybir.dt.float32r
I8 = mybir.dt.int8
I32 = mybir.dt.int32
AX = mybir.AxisListType

P = 128
SEQ = 256
D = 128
HEADS, DH = 16, 64
PAIRS = HEADS // 2
CH = HEADS * DH
E, DFF = 8, 512
FB = DFF // P
EPS = 1e-5
GT = 512
LOGIT_MIN = -3.5
LEVELS = [16, 8, 4, 2, 1]
MID, S32, S64, S128 = 0, SEQ, SEQ + SEQ // 2, 2 * SEQ
VER = 5 * SEQ // 2
NEG = -3.0e38


def build(nc, x, w_in, w_out, b_in, b_v, cols, alpha, alpha_row, w1, w2, w_router, out):
    T = x.shape[0]
    NT = T // P
    G = T // GT
    TG = GT // P
    NB = GT // SEQ

    outer = ExitStack()
    with outer:
        def sb(name, shape, dt=F32, ctx=outer):
            return ctx.enter_context(nc.sbuf_tensor(name, shape, dt))

        def sem(name, ctx=outer):
            return ctx.enter_context(nc.semaphore(name))

        x_all = sb("x_all", [P, NT, D])
        u_all = sb("u_all", [P, NT, D])
        ident = sb("ident", [P, P])
        w1_hi = sb("w1_hi", [P, E, FB, P], F32R)
        w1_lo = sb("w1_lo", [P, E, FB, P], F32R)
        w2_hi = sb("w2_hi", [P, E, FB, P], F32R)
        w2_lo = sb("w2_lo", [P, E, FB, P], F32R)
        wr_sb = sb("wr_sb", [P, E])
        ffn_split = sem("ffn_split")
        ident_ready = sem("ident_ready")

        attention(nc, sb, sem, x, w_in, w_out, b_in, b_v, cols, alpha, alpha_row, w1, w2, w_router,
                  x_all, u_all, ident, ident_ready,
                  (w1_hi, w1_lo, w2_hi, w2_lo), wr_sb, ffn_split, NT, G, TG, NB)
        experts(nc, sb, sem, out, x_all, u_all, ident,
                (w1_hi, w1_lo, w2_hi, w2_lo), wr_sb, NT, G, TG)


def attention(nc, sb_, sem_, x, w_in, w_out, b_in, b_v, cols, alpha, alpha_row, w1, w2, w_router,
              x_all, u_all, ident, ident_ready, ffn_w, wr_sb,
              ffn_split, NT, G, TG, NB):
    ctx = ExitStack()
    with ctx:
        def sb(name, shape, dt=F32):
            return sb_(name, shape, dt, ctx)

        def sem(name):
            return sem_(name, ctx)

        wi_hi = sb("wi_hi", [P, 4, CH], F32R)
        wi_lo = sb("wi_lo", [P, 4, CH], F32R)
        wo_hi = sb("wo_hi", [P, PAIRS, D], F32R)
        wo_lo = sb("wo_lo", [P, PAIRS, D], F32R)
        STG, CHUNK = 2, 512
        stage = sb("stage", [P, STG, CHUNK])
        bi = sb("bi", [P, 3, PAIRS])
        bv = sb("bv", [P, CH])
        col = sb("col", [P, 3])
        al = sb("al", [P, PAIRS])
        al_min = sb("al_min", [1, 1])
        narrow = sb("narrow", [1, 1], I32)
        pow_up = sb("pow_up", [P, PAIRS, 129])
        pow_dn = sb("pow_dn", [P, PAIRS, 129])
        mid_q = sb("mid_q", [P, PAIRS, 32])
        mid_k = sb("mid_k", [P, PAIRS, 32])
        mask = sb("mask", [P, 1 + len(LEVELS), 3, P], I8)
        xn = sb("xn", [P, GT])
        xn_hi = sb("xn_hi", [P, GT], F32R)
        xn_lo = sb("xn_lo", [P, GT], F32R)
        v_sb = sb("v_sb", [P, TG, CH])
        q_raw = sb("q_raw", [P, GT])
        k_raw = sb("k_raw", [P, GT])
        gate = sb("gate", [P, 2, GT])
        qv = sb("qv", [P, 2, NB, VER])
        kv = sb("kv", [P, 2, NB, VER])
        a_sb = sb("a_sb", [P, NB, 2, 3 * P])
        og = sb("og", [P, GT])
        z = sb("z", [P, TG, D])
        stats = sb("stats", [P, TG, 6])
        mv = sb("mv", [P, TG, 2])
        std = sb("std", [P, TG])
        rstd = sb("rstd", [P, TG])
        mv3 = sb("mv3", [P, TG, 2])
        std3 = sb("std3", [P, TG])
        rstd3 = sb("rstd3", [P, TG])
        eps_col = sb("eps_col", [P, 1])
        og_hi = sb("og_hi", [P, GT], F32R)
        og_lo = sb("og_lo", [P, GT], F32R)
        y_sb = sb("y_sb", [P, GT])

        al_row = v_sb[0:1, 0, :]
        it = q_raw[:, 0:2 * P].bitcast(I32).rearrange("p (a q) -> p a q", a=2)
        ring = ctx.enter_context(nc.psum_tensor("ring", [P, 2, 512], F32))
        sc = ctx.enter_context(nc.psum_tensor("sc", [P, NB, 2, 512], F32))
        ps_o = ctx.enter_context(nc.psum_tensor("ps_o", [P, 512], F32))
        ps_y = ctx.enter_context(nc.psum_tensor("ps_y", [P, 512], F32))

        x0_in = sem("x0_in")
        x_loaded = sem("x_loaded")
        small_in = sem("small_in")
        al_in = sem("al_in")
        hi_done = sem("hi_done")
        lo_done = sem("lo_done")
        stats_done = sem("stats_done")
        std_done = sem("std_done")
        stats3_done = sem("stats3_done")
        std3_done = sem("std3_done")
        zeros_ready = sem("zeros_ready")
        norm_turn = sem("norm_turn")
        sig_done = sem("sig_done")
        dve_step = sem("dve_step")
        mask_ready = sem("mask_ready")
        narrow_ready = sem("narrow_ready")
        z_ready = sem("z_ready")
        u_step = sem("u_step")
        xn_raw = sem("xn_raw")
        xn_ready = sem("xn_ready")
        v_ready = sem("v_ready")
        ring_full = [sem(f"ring_full{r}") for r in range(2)]
        raw_ready = sem("raw_ready")
        ver_ready = sem("ver_ready")
        gate_ready = sem("gate_ready")
        sc_done = sem("sc_done")
        keep_turn = sem("keep_turn")
        a_ready = sem("a_ready")
        out_done = sem("out_done")
        o_read = sem("o_read")
        og_raw = sem("og_raw")
        og_ready = sem("og_ready")
        wo_done = sem("wo_done")
        y_ready = sem("y_ready")
        lv_ready = sem("lv_ready")
        xn_step = sem("xn_step")
        iota_ready = sem("iota_ready")
        y_read = sem("y_read")
        stage_in = [sem(f"stage_in{i}") for i in range(STG)]

        wi_h, wi_l = [w[:].rearrange("p a c -> p (a c)") for w in (wi_hi, wi_lo)]
        wo_h, wo_l = [w[:].rearrange("p a c -> p (a c)") for w in (wo_hi, wo_lo)]
        f_h = [w[:].rearrange("p e b c -> p (e b c)") for w in (ffn_w[0], ffn_w[2])]
        f_l = [w[:].rearrange("p e b c -> p (e b c)") for w in (ffn_w[1], ffn_w[3])]
        chunks = [(w_in, wi_h, wi_l, j * CH) for j in (3, 0, 1, 2)]
        chunks += [(w_out, wo_h, wo_l, c) for c in range(0, CH, CHUNK)]
        chunks += [(w_in, wi_h, wi_l, j * CH + CHUNK) for j in (3, 0, 1, 2)]
        FIRST = len(chunks)
        for i, src in enumerate((w1, w2)):
            chunks += [(src, f_h[i], f_l[i], c * CHUNK) for c in range(E * DFF // CHUNK)]
        lands = [(t[:, 0], half) for t in (qv, kv) for half in range(2)] + [None] * (CH // CHUNK)
        lands += [(t[:, 1], half) for t in (qv, kv) for half in range(2)]
        lands += [None] * (len(chunks) - FIRST)
        staged, landing, arrival = [], [], []
        for n in range(len(chunks)):
            if lands[n]:
                t, half = lands[n]
                landing.append(t.rearrange("p b v -> p (b v)")[:, half * CHUNK:(half + 1) * CHUNK])
                arrival.append((sem(f"chunk_in{n}"), 16))
            else:
                landing.append(stage[:, len(staged) % STG, :])
                arrival.append((stage_in[len(staged) % STG], 16 * (len(staged) // STG + 1)))
                staged.append(n)

        start_uses = [("turn_z", 0)] + [("v", t) for t in range(TG)] + [("proj", 0, j) for j in range(3)]
        body_uses = []
        for p in range(PAIRS - 1):
            body_uses += [("proj", p + 1, j) for j in range(3)]
            if p < TG:
                body_uses.append(("v", TG + p))
        LAST_USES = len(body_uses) + 1
        ahead = len(body_uses)
        body_uses += start_uses + [("turn_y",)]
        assert len(start_uses) % 2 == 0 and len(body_uses) % 2 == 0

        def use_of(kind, own=True):
            if not own:
                return ahead + start_uses.index(kind)
            return LAST_USES - 1 if kind == ("last_y",) else body_uses.index(kind)

        def full_at(i, g):
            return i // 2 + 1 if g is None else len(start_uses) // 2 + g * (len(body_uses) // 2) + i // 2 + 1

        def read_by(kind, g):
            if kind[0] == "turn_z":
                return xn_raw, g + 1
            if kind[0] == "v":
                return v_ready, 2 * TG * g + kind[1] + 1
            if kind[0] == "turn_y":
                return y_read, 1 + g + 1
            _, p, j = kind
            return (raw_ready, 2 * (PAIRS * g + p) + j + 1) if j < 2 else (gate_ready, PAIRS * g + p + 1)

        block = ctx.enter_context(nc.Block())

        @block.sync
        def _(sp):
            xv = x.rearrange("(t p) d -> p t d", p=P)

            def rows_in(g):
                sp.dma_start(x_all[:, g * TG:(g + 1) * TG, :], xv[:, g * TG:(g + 1) * TG, :])\
                  .then_inc(x0_in if g == 0 else x_loaded, 16)

            rows_in(0)
            for n, (src, _, _, c) in enumerate(chunks):
                if n == FIRST:
                    for g in range(1, G):
                        rows_in(g)
                if n in staged and staged.index(n) >= STG:
                    sp.wait_ge(lo_done, staged[staged.index(n) - STG] + 1)
                sp.dma_start(landing[n], src[:, c:c + CHUNK]).then_inc(arrival[n][0], 16)

        @block.gpsimd
        def _(pool):
            nc.gpsimd.memset(ident[:], 1.0).then_inc(mask_ready, 1)
            causal = k_raw[:, 0:3 * P].rearrange("p (t q) -> p t q", t=3)
            nc.gpsimd.memset(causal, 1.0).then_inc(mask_ready, 1)
            pool.wait_ge(mask_ready, 2)
            nc.gpsimd.affine_select(out=ident[:], in_=ident[:], compare_op=ALU.is_equal, fill=0.0, base=0,
                                    pattern=[[1, P]], channel_multiplier=-1).then_inc(ident_ready, 1)
            for t in (0, 2):
                nc.gpsimd.affine_select(out=causal[:, t, :], in_=causal[:, t, :], compare_op=ALU.is_ge, fill=0.0,
                                        base=0, pattern=[[1, P]], channel_multiplier=-1).then_inc(mask_ready, 1)
            nc.gpsimd.iota(it[:, 0, :], pattern=[[1, P]], base=0, channel_multiplier=0).then_inc(iota_ready, 1)
            nc.gpsimd.iota(it[:, 1, :], pattern=[[0, P]], base=0, channel_multiplier=1).then_inc(iota_ready, 1)
            nc.gpsimd.memset(a_sb[:], 0.0).then_inc(zeros_ready, 1)
            for n, (_, hi, lo, c) in enumerate(chunks):
                h, l = hi[:, c:c + CHUNK], lo[:, c:c + CHUNK]
                if n < FIRST:
                    pool.wait_ge(hi_done, n + 1)
                else:
                    pool.wait_ge(*arrival[n])
                    nc.gpsimd.tensor_copy(h, landing[n]).then_inc(ffn_split, 1)
                    pool.wait_ge(ffn_split, n - FIRST + 1)
                nc.gpsimd.tensor_tensor(l, landing[n], h.bitcast(F32), ALU.subtract).then_inc(lo_done, 1)

        @block.scalar
        def _(act):
            act.dma_start(al[:], alpha).then_inc(al_in, 16)
            act.dma_start(col[:], cols).then_inc(small_in, 16)
            act.dma_start(al_row, alpha_row).then_inc(small_in, 16)
            act.dma_start(bv[:], b_v.to_broadcast([P, CH])).then_inc(small_in, 16)
            act.dma_start(bi[:], b_in).then_inc(small_in, 16)
            act.dma_start(wr_sb[:], w_router).then_inc(small_in, 16)
            act.wait_ge(al_in, 16)
            nc.scalar.activation(pow_up[:, :, 1], al[:], ACT.Sigmoid).then_inc(sig_done, 1)

            def high(n):
                _, hi, _, c = chunks[n]
                act.wait_ge(*arrival[n])
                nc.scalar.activation(hi[:, c:c + CHUNK], landing[n], ACT.Copy).then_inc(hi_done, 1)

            def deviations(g, which):
                act.wait_ge(stats_done, 2 * g + which + 1)
                nc.scalar.activation(std[:], mv[:, :, 1], ACT.Sqrt, bias=eps_col[:, 0:1])\
                  .then_inc(std_done, 1)

            def filled(i, g):
                act.wait_ge(ring_full[i % 2], full_at(i, g))
                return ring[:, i % 2, :]

            def xn_out(g, i, at):
                src = filled(i, at)
                nc.scalar.activation(xn[:], src, ACT.Identity, bias=col[:, 2:3], scale=col[:, 1:2])\
                  .then_inc(xn_raw, 1)

            def evac_qk(p, g, uses, at):
                for j, dst in enumerate((q_raw, k_raw)):
                    src = filled(uses[j], at)
                    act.wait_ge(ver_ready, 2 * (PAIRS * g + p) + j + 1)
                    nc.scalar.activation(dst[:], src, ACT.Identity, bias=bi[:, j, p:p + 1]).then_inc(raw_ready, 1)

            def evac_gate(p, g, uses, at):
                src = filled(uses[2], at)
                act.wait_ge(og_ready, PAIRS * g + p + 1)
                nc.scalar.activation(gate[:, p % 2, :], src, ACT.Silu, bias=bi[:, 2, p:p + 1])\
                  .then_inc(gate_ready, 1)

            def uses_of(p, own=True):
                return [use_of(("proj", p, j), own) for j in range(3)]

            deviations(0, 0)
            high(0)
            deviations(0, 1)
            for n in range(1, 4):
                high(n)
            act.wait_ge(small_in, 5 * 16)
            xn_out(0, 0, None)
            for n in range(4, FIRST):
                high(n)
            first_uses = [start_uses.index(("proj", 0, j)) for j in range(3)]
            evac_qk(0, 0, first_uses, None)
            evac_gate(0, 0, first_uses, None)
            evac_qk(1, 0, uses_of(1), 0)
            evac_gate(1, 0, uses_of(1), 0)

            def body(g, last):
                for p in range(2, PAIRS):
                    evac_qk(p, g, uses_of(p), g)
                    evac_gate(p, g, uses_of(p), g)
                    if not last and p in (3, 4):
                        deviations(g + 1, p - 3)
                if not last:
                    xn_out(g + 1, use_of(("turn_z", 0), False), g)
                    ahead_uses = uses_of(0, False)
                    evac_qk(0, g + 1, ahead_uses, g)
                    evac_gate(0, g + 1, ahead_uses, g)
                act.wait_ge(wo_done, 1 + PAIRS * g + PAIRS)
                nc.scalar.activation(y_sb[:], ps_y[:], ACT.Identity, bias=col[:, 0:1]).then_inc(y_ready, 1)
                if not last:
                    evac_qk(1, g + 1, uses_of(1), g + 1)
                act.wait_ge(stats3_done, g + 1)
                nc.scalar.activation(std3[:], mv3[:, :, 1], ACT.Sqrt, bias=eps_col[:, 0:1]).then_inc(std3_done, 1)
                if not last:
                    evac_gate(1, g + 1, uses_of(1), g + 1)

            with act.Fori(0, G - 1) as g:
                body(g, False)
            body(G - 1, True)

        @block.tensor
        def _(pe):
            def three(dst, w_hi, w_lo, x_hi, x_lo, start=True, stop=True):
                nc.tensor.matmul(dst, w_hi, x_hi, start=start, stop=False)
                nc.tensor.matmul(dst, w_hi, x_lo, start=False, stop=False)
                return nc.tensor.matmul(dst, w_lo, x_hi, start=False, stop=stop)

            def at(i, before=None):
                if before:
                    pe.wait_ge(*before)
                return ring[:, i % 2, :], ring_full[i % 2]

            def turn(dst, full, src):
                for t in range(TG):
                    mm = nc.tensor.transpose(dst[:, t * P:(t + 1) * P], src[:, t * P:(t + 1) * P], ident[:])
                mm.then_inc(full, 1)

            def value(use, bank):
                dst, full = bank
                h, t = divmod(use, TG)
                rows, c = slice(t * P, (t + 1) * P), slice(h * 512, (h + 1) * 512)
                three(dst, xn_hi[:, rows], xn_lo[:, rows], wi_hi[:, 3, c], wi_lo[:, 3, c]).then_inc(full, 1)

            def proj(p, j, bank):
                dst, full = bank
                c = slice(p * P, (p + 1) * P)
                three(dst, wi_hi[:, j, c], wi_lo[:, j, c], xn_hi[:], xn_lo[:]).then_inc(full, 1)

            z_flat = z[:].rearrange("p t d -> p (t d)")

            def body(g, last, levels):
                R = 1 + len(levels)

                def claim(kind, own=True):
                    i = use_of(kind, own)
                    if i == 0:
                        before = gate_ready, PAIRS * g + 1
                    elif i == 1:
                        before = y_read, g + 1
                    else:
                        before = read_by(body_uses[i - 2], g + 1 if i - 2 >= ahead else g)
                    return at(i, before)

                def diagonal(p, b, r, c0):
                    h = slice(r * DH, (r + 1) * DH)
                    for t in range(2):
                        mm = nc.tensor.matmul(sc[:, b, r, 2 * t * P:2 * t * P + P],
                                              kv[h, p % 2, b, c0 + t * P:c0 + (t + 1) * P],
                                              qv[h, p % 2, b, c0 + t * P:c0 + (t + 1) * P],
                                              start=True, stop=True)
                    return mm

                def scores(p, b):
                    n = PAIRS * g + p
                    pe.wait_ge(ver_ready, 2 + 2 * n + 2)
                    pe.wait_ge(a_ready, 2 * R * n + b + 1)
                    for r in range(2):
                        diagonal(p, b, r, MID)
                    for r in range(2):
                        h = slice(r * DH, (r + 1) * DH)
                        for t in range(2):
                            for L, c in ((32, S32), (64, S64)):
                                for i in range(64 // L):
                                    s0 = c + 64 * t + i * L
                                    key = 2 * L * i
                                    q0 = 2 * t * P + key + L
                                    nc.tensor.matmul(sc[key:key + L, b, r, q0:q0 + L], kv[h, p % 2, b, s0:s0 + L],
                                                     qv[h, p % 2, b, s0:s0 + L], start=True, stop=True)
                        mm = nc.tensor.matmul(sc[:, b, r, P:2 * P], kv[h, p % 2, b, S128:S128 + P],
                                              qv[h, p % 2, b, S128:S128 + P], start=True, stop=True)
                    mm.then_inc(sc_done, 1)

                def finer(p):
                    n = PAIRS * g + p
                    for i, L in enumerate(levels):
                        pe.wait_ge(lv_ready, len(levels) * n + i + 1)
                        for b in range(NB):
                            pe.wait_ge(a_ready, 2 * R * n + 2 * (i + 1) + b + 1)
                            for r in range(2):
                                mm = diagonal(p, b, r, S32)
                            mm.then_inc(sc_done, 1)

                def outs(p):
                    n = PAIRS * g + p
                    if p == 0:
                        pe.wait_ge(v_ready, 2 * TG * g + TG)
                    if p == PAIRS // 2:
                        pe.wait_ge(v_ready, 2 * TG * g + 2 * TG)
                    pe.wait_ge(o_read, n + 1)
                    for b in range(NB):
                        pe.wait_ge(a_ready, 2 + 2 * R * n + 2 * (R - 1) + b + 1)
                        dst = ps_o[:, b * SEQ:(b + 1) * SEQ]
                        c = [slice(p * P + r * DH, p * P + (r + 1) * DH) for r in range(2)]
                        for r in range(2):
                            nc.tensor.matmul(dst[r * DH:(r + 1) * DH, :], v_sb[:, 2 * b, c[r]],
                                             a_sb[:, b, r, 0:2 * P], start=True, stop=False,
                                             skip_group_check=True)
                        for r in range(2):
                            mm = nc.tensor.matmul(dst[r * DH:(r + 1) * DH, P:2 * P], v_sb[:, 2 * b + 1, c[r]],
                                                  a_sb[:, b, r, 2 * P:3 * P], start=False, stop=True,
                                                  skip_group_check=True)
                        mm.then_inc(out_done, 1)

                def project_out(p):
                    n = PAIRS * g + p
                    pe.wait_ge(og_ready, 2 + n + 1)
                    three(ps_y[:], wo_hi[:, p, :], wo_lo[:, p, :], og_hi[:], og_lo[:], start=(p == 0),
                          stop=(p == PAIRS - 1)).then_inc(wo_done, 1)

                for p in range(PAIRS):
                    if p + 1 < PAIRS:
                        for j in range(2):
                            proj(p + 1, j, claim(("proj", p + 1, j)))
                    scores(p, 0)
                    if p + 1 < PAIRS:
                        proj(p + 1, 2, claim(("proj", p + 1, 2)))
                    scores(p, 1)
                    finer(p)
                    if p == 0:
                        pe.wait_ge(lo_done, FIRST)
                    if p < TG:
                        value(TG + p, claim(("v", TG + p)))
                    if p == PAIRS - 1 and not last:
                        pe.wait_ge(xn_ready, g + 2)
                        for t in range(TG // 2):
                            value(t, claim(("v", t), False))
                    if p:
                        project_out(p - 1)
                    outs(p)
                    if p == PAIRS - 2 and not last:
                        bank = claim(("turn_z", 0), False)
                        pe.wait_ge(z_ready, g + 2)
                        turn(*bank, z_flat)
                if not last:
                    for t in range(TG // 2, TG):
                        value(t, claim(("v", t), False))
                    for j in range(3):
                        proj(0, j, claim(("proj", 0, j), False))
                project_out(PAIRS - 1)
                bank = claim(("last_y",) if last else ("turn_y",))
                pe.wait_ge(y_ready, g + 1)
                turn(*bank, y_sb)

            def groups(levels):
                pe.sem_inc(sc_done, 2 * (1 + len(levels)) + 1)
                with pe.Fori(0, G - 1) as g:
                    body(g, False, levels)
                body(G - 1, True, levels)

            def start_claim(i):
                return at(i, read_by(start_uses[i - 2], 0) if i >= 2 else None)

            pe.wait_ge(ident_ready, 1)
            pe.wait_ge(z_ready, 1)
            turn(*start_claim(0), z_flat)
            pe.wait_ge(xn_ready, 1)
            pe.wait_ge(lo_done, 1)
            for t in range(TG):
                value(t, start_claim(1 + t))
            for j in range(3):
                pe.wait_ge(lo_done, 2 + j)
                proj(0, j, start_claim(1 + TG + j))
            pe.sem_inc(out_done, 2)
            pe.sem_inc(wo_done, 1)
            pe.wait_ge(narrow_ready, 1)
            small_logit = pe.value_load(narrow[0:1, 0:1], min_val=0, max_val=1)
            with pe.If(small_logit):
                groups(LEVELS)
            with pe.Else():
                groups([])

        @block.vector
        def _(dve):
            step = [0]

            def chain(ins):
                step[0] += 1
                ins.then_inc(dve_step, 1)
                dve.wait_ge(dve_step, step[0])

            def rows_of(buf, g, t):
                return buf[:, bass.ds(g * TG + t, 1), :].rearrange("p a d -> p (a d)")

            def moments(src, g, mv_, link):
                dve.sem_inc(norm_turn, 1)
                for t in range(TG):
                    last = nc.vector.bn_stats(stats[:, t, :], rows_of(src, g, t))
                link(last)
                dve.sem_inc(norm_turn, 1)
                for t in range(TG):
                    last = nc.vector.bn_aggr(mv_[:, t, :], stats[:, t, :])
                return last

            def normalised(dst, src, g, mv_, std_, rstd_, link):
                link(nc.vector.reciprocal(rstd_[:], std_[:]))
                for t in range(TG):
                    last = nc.vector.tensor_scalar(dst(t), rows_of(src, g, t), mv_[:, t, 0:1], rstd_[:, t:t + 1],
                                                   ALU.subtract, ALU.mult)
                return last

            def rows_a(g, link):
                if link is not chain:
                    dve.wait_ge(z_ready, g)
                moments(x_all, g, mv, link).then_inc(stats_done, 1)

            def rows_b(g, link):
                dve.wait_ge(std_done, 2 * g + 1)
                link(normalised(lambda t: rows_of(u_all, g, t), x_all, g, mv, std, rstd, link))
                moments(u_all, g, mv, link).then_inc(stats_done, 1)

            def rows_c(g, link):
                dve.wait_ge(std_done, 2 * g + 2)
                normalised(lambda t: z[:, t, :], u_all, g, mv, std, rstd, link).then_inc(z_ready, 1)
                r = bass.ds(g * TG, TG)
                link(nc.vector.tensor_tensor(x_all[:, r, :], x_all[:, r, :], u_all[:, r, :], ALU.add))

            def split_xn(g):
                dve.wait_ge(xn_raw, g + 1)
                nc.vector.tensor_copy(xn_hi[:], xn[:]).then_inc(xn_step, 1)
                dve.wait_ge(xn_step, g + 1)
                nc.vector.tensor_tensor(xn_lo[:], xn[:], xn_hi[:].bitcast(F32), ALU.subtract).then_inc(xn_ready, 1)

            def filled(i, g):
                dve.wait_ge(ring_full[i % 2], full_at(i, g))
                return ring[:, i % 2, :]

            def value_out(use, src):
                h, t = divmod(use, TG)
                c = slice(h * 512, (h + 1) * 512)
                nc.vector.tensor_tensor(v_sb[:, t, c], src, bv[:, c], ALU.add).then_inc(v_ready, 1)

            def doubled(ks):
                for k in ks:
                    a_k = pow_up[:, :, k:k + 1].to_broadcast([P, PAIRS, k])
                    nc.vector.tensor_tensor(pow_up[:, :, k + 1:2 * k + 1], pow_up[:, :, 1:k + 1], a_k, ALU.mult)
                    chain(nc.vector.tensor_tensor(pow_dn[:, :, 128 - 2 * k:128 - k], pow_dn[:, :, 128 - k:128],
                                                  a_k, ALU.mult))

            nc.vector.memset(eps_col[:], EPS)
            nc.vector.memset(pow_up[:, :, 0], 1.0)
            chain(nc.vector.memset(pow_dn[:, :, 128], 1.0))
            dve.wait_ge(x0_in, 16)
            rows_a(0, chain)
            dve.wait_ge(sig_done, 1)
            chain(nc.vector.tensor_copy(pow_dn[:, :, 127], pow_up[:, :, 1]))
            doubled([1, 2, 4, 8])
            rows_b(0, chain)
            doubled([16, 32])
            rows_c(0, chain)
            dve.wait_ge(small_in, 5 * 16)
            chain(nc.vector.tensor_reduce(al_min[:], al_row, AX.X, ALU.min))
            nc.vector.tensor_scalar(narrow[:], al_min[:], LOGIT_MIN, None, ALU.is_lt).then_inc(narrow_ready, 1)
            split_xn(0)
            nc.vector.tensor_copy(mid_q[:, :, 16:32], pow_up[:, :, 0:16])
            nc.vector.tensor_copy(mid_k[:, :, 0:16], pow_dn[:, :, 112:128])
            for t in range(TG):
                value_out(t, filled(1 + t, None))
            doubled([64])
            nc.vector.reciprocal(mid_q[:, :, 0:16], pow_dn[:, :, 112:128])
            nc.vector.reciprocal(mid_k[:, :, 16:32], pow_up[:, :, 0:16])
            dve.sem_inc(a_ready, 2)
            dve.sem_inc(o_read, 1)
            dve.sem_inc(y_read, 1)
            dve.sem_inc(og_ready, 2)
            dve.wait_ge(mask_ready, 4)
            dve.wait_ge(zeros_ready, 1)

            def groups(levels):
                R = 1 + len(levels)

                def decayed(dst, raw, p, odd, tab_mid, tab):
                    def spans(L):
                        return raw[:].rearrange("c (b n o l) -> c b n o l", b=NB, o=2, l=L)[:, :, :, odd, :]

                    if R == 1:
                        nc.vector.tensor_tensor(
                            dst[:, p % 2, :, MID:S32].rearrange("c b (n l) -> c b n l", l=32),
                            raw[:].rearrange("c (b n l) -> c b n l", b=NB, l=32),
                            tab_mid[:, p:p + 1, :].unsqueeze(1).to_broadcast([P, NB, SEQ // 32, 32]),
                            ALU.mult)
                    else:
                        nc.vector.tensor_copy(dst[:, p % 2, :, MID:S32],
                                              raw[:].rearrange("c (b n) -> c b n", b=NB))
                    for L, c in ((32, S32), (64, S64), (128, S128)):
                        n = SEQ // (2 * L)
                        last = nc.vector.tensor_tensor(
                            dst[:, p % 2, :, c:c + P].rearrange("c b (n l) -> c b n l", l=L), spans(L),
                            tab(p, L).unsqueeze(1).to_broadcast([P, NB, n, L]), ALU.mult)
                    return last

                def up(p, L):
                    return pow_up[:, p:p + 1, 0:L]

                def down(p, L):
                    return pow_dn[:, p:p + 1, P - L:P]

                def versions(p, g):
                    n = PAIRS * g + p
                    dve.wait_ge(sc_done, 2 * R * n + 1)
                    dve.wait_ge(raw_ready, 2 * n + 1)
                    decayed(qv, q_raw, p, 1, mid_q, up).then_inc(ver_ready, 1)
                    dve.wait_ge(raw_ready, 2 * n + 2)
                    decayed(kv, k_raw, p, 0, mid_k, down).then_inc(ver_ready, 1)

                def keep(b, i):
                    m = mask[:, i, :, :].rearrange("p t q -> p (t q)").unsqueeze(1)
                    dve.sem_inc(keep_turn, 1)
                    nc.vector.copy_predicated(a_sb[:, b, :, :], m.to_broadcast([P, 2, 3 * P]),
                                              sc[:, b, :, 0:3 * P]).then_inc(a_ready, 1)

                def level(dst, p, tab, L):
                    return nc.vector.tensor_tensor(
                        dst[:, p % 2, :, S32:S32 + SEQ].rearrange("c b (n l) -> c b n l", l=L),
                        dst[:, p % 2, :, MID:MID + SEQ].rearrange("c b (n l) -> c b n l", l=L),
                        tab(p, L).unsqueeze(1).to_broadcast([P, NB, SEQ // L, L]), ALU.mult)

                def masked(p, g):
                    n = PAIRS * g + p
                    for b in range(NB):
                        dve.wait_ge(sc_done, 2 * R + 1 + 2 * R * n + b + 1)
                        dve.wait_ge(out_done, 2 * n + b + 1)
                        keep(b, 0)
                    for i, L in enumerate(levels):
                        level(qv, p, up, L)
                        level(kv, p, down, L).then_inc(lv_ready, 1)
                        for b in range(NB):
                            dve.wait_ge(sc_done, 2 * R + 1 + 2 * R * n + 2 * (i + 1) + b + 1)
                            keep(b, 1 + i)

                def gated(p, g):
                    n = PAIRS * g + p
                    dve.wait_ge(out_done, 2 + 2 * n + 2)
                    dve.wait_ge(gate_ready, n + 1)
                    nc.vector.tensor_tensor(og[:], ps_o[:], gate[:, p % 2, :], ALU.mult).then_inc(o_read, 1)
                    dve.wait_ge(o_read, 1 + n + 1)
                    dve.wait_ge(wo_done, n + 1)
                    nc.vector.tensor_copy(og_hi[:], og[:]).then_inc(og_raw, 1)
                    dve.wait_ge(og_raw, n + 1)
                    nc.vector.tensor_tensor(og_lo[:], og[:], og_hi[:].bitcast(F32), ALU.subtract)\
                      .then_inc(og_ready, 1)

                STEPS = 9

                def body(g, last):
                    done = [0]

                    def link(ins):
                        done[0] += 1
                        ins.then_inc(u_step, 1)
                        dve.wait_ge(u_step, STEPS * g + done[0])

                    for p in range(PAIRS):
                        if 1 <= p < PAIRS - 1:
                            versions(p + 1, g)
                        if not last and p in (2, 3, 4):
                            if p == 2:
                                dve.wait_ge(x_loaded, 16 * (G - 1))
                            (rows_a, rows_b, rows_c)[p - 2](g + 1, link)
                        masked(p, g)
                        if p < TG:
                            value_out(TG + p, filled(use_of(("v", TG + p)), g))
                        if p == PAIRS - 1 and not last:
                            for t in range(TG // 2):
                                value_out(t, filled(use_of(("v", t), False), g))
                        gated(p, g)
                        if p == PAIRS - 2 and not last:
                            split_xn(g + 1)
                    if not last:
                        for t in range(TG // 2, TG):
                            value_out(t, filled(use_of(("v", t), False), g))
                        versions(0, g + 1)
                    src = filled(use_of(("last_y",) if last else ("turn_y",)), g)
                    r = bass.ds(g * TG, TG)
                    nc.vector.tensor_tensor(x_all[:, r, :], src.rearrange("p (t d) -> p t d", t=TG),
                                            x_all[:, r, :], ALU.add).then_inc(y_read, 1)
                    dve.wait_ge(y_read, 1 + g + 1)
                    moments(x_all, g, mv3, link).then_inc(stats3_done, 1)
                    if not last:
                        versions(1, g + 1)
                    dve.wait_ge(std3_done, g + 1)
                    link(normalised(lambda t: rows_of(u_all, g, t), x_all, g, mv3, std3, rstd3, link))
                    assert done[0] == (3 if last else STEPS), done

                dve.sem_inc(ver_ready, 2)
                versions(0, 0)
                dve.wait_ge(lo_done, FIRST)
                versions(1, 0)
                with dve.Fori(0, G - 1) as g:
                    body(g, False)
                body(G - 1, True)

            causal = k_raw[:, 0:3 * P].rearrange("p (t q) -> p t q", t=3)

            def general_masks():
                nc.vector.tensor_copy(mask[:, 0, :, :], causal)
                nc.vector.memset(mask[:, 1:, 1, :], 0)
                dve.wait_ge(iota_ready, 2)
                apart, test = og[:, 0:P], og[:, P:2 * P]
                xor = og[:, 2 * P:3 * P].bitcast(I32)
                chain(nc.vector.tensor_tensor(xor, it[:, 0, :], it[:, 1, :], ALU.bitwise_xor))
                chain(nc.vector.tensor_copy(apart, xor))
                for i, L in enumerate(LEVELS):
                    chain(nc.vector.tensor_scalar(test, apart, float(L), None, ALU.is_ge))
                    chain(nc.vector.scalar_tensor_tensor(out=test, in0=apart, scalar=float(2 * L), in1=test,
                                                         op0=ALU.is_lt, op1=ALU.mult))
                    for t in (0, 2):
                        last = nc.vector.tensor_tensor(mask[:, 1 + i, t, :], test, causal[:, t, :], ALU.mult)
                    chain(last)
                chain(nc.vector.tensor_scalar(test, apart, 32.0, None, ALU.is_ge))
                chain(nc.vector.scalar_tensor_tensor(out=test, in0=apart, scalar=0.0, in1=test,
                                                     op0=ALU.is_equal, op1=ALU.add))
                for t in (0, 2):
                    last = nc.vector.tensor_tensor(mask[:, 0, t, :], test, causal[:, t, :], ALU.mult)
                chain(last)

            small_logit = dve.value_load(narrow[0:1, 0:1], min_val=0, max_val=1)
            before_masks = step[0]
            with dve.If(small_logit):
                general_masks()
                groups(LEVELS)
            with dve.Else():
                step[0] = before_masks
                chain(nc.vector.tensor_copy(mask[:, 0, :, :], causal))
                groups([])


def experts(nc, sb_, sem_, out, x_all, u_all, ident, ffn_w, wr_sb, NT, G, TG):
    T = NT * P
    HR = 4
    K = E * FB
    ctx = ExitStack()
    with ctx:
        def sb(name, shape, dt=F32):
            return sb_(name, shape, dt, ctx)

        def sem(name):
            return sem_(name, ctx)

        xt = sb("xt", [P, T])
        xt_hi = sb("xt_hi", [P, T], F32R)
        xt_lo = sb("xt_lo", [P, T], F32R)
        lg = sb("lg", [P, NT, E])
        ex = sb("ex", [P, NT, E])
        cand = sb("cand", [P, NT, E])
        first = sb("first", [P, NT, E])
        second = sb("second", [P, NT, E])
        rest = sb("rest", [P, NT, E])
        red = sb("red", [P, NT])
        rank = sb("rank", [P, E])
        gates = sb("gates", [P, NT, 64], F32R)
        gates_t = sb("gates_t", [64, T], F32R)
        pick_f = sb("pick_f", [64, E, P])
        pick = sb("pick", [64, E, P], F32R)
        h = sb("h", [P, 2, GT])
        h_hi = sb("h_hi", [P, HR, GT], F32R)
        h_lo = sb("h_lo", [P, HR, GT], F32R)
        gb = sb("gb", [P, 2, GT])
        part = sb("part", [P, GT])
        acc = sb("acc", [P, GT])
        ps = ctx.enter_context(nc.psum_tensor("ps", [P, 8, 512], F32))
        Y, GB, TR = 4, 6, 7

        dve_step2 = sem("dve_step2")
        turned = sem("turned")
        xt_ready = sem("xt_ready")
        xt_split = sem("xt_split")
        logits_done = sem("logits_done")
        centred = sem("centred")
        exp_done = sem("exp_done")
        rank_ready = sem("rank_ready")
        pick_ready = sem("pick_ready")
        pick_split = sem("pick_split")
        gates_ready = sem("gates_ready")
        gates_turned = sem("gates_turned")
        gates_t_ready = sem("gates_t_ready")
        h_full = sem("h_full")
        h_act = sem("h_act")
        h_hi_done = sem("h_hi_done")
        h_split = sem("h_split")
        y_step = sem("y_step")
        gb_full = sem("gb_full")
        gb_turn = sem("gb_turn")
        gb_ready = sem("gb_ready")
        y_used = sem("y_used")
        acc_step = sem("acc_step")
        acc_turned = sem("acc_turned")
        out_ready = sem("out_ready")
        out_sent = sem("out_sent")
        block = ctx.enter_context(nc.Block())

        @block.sync
        def _(sp):
            ov = out.rearrange("(t p) d -> p t d", p=P)
            for g in range(G):
                sp.wait_ge(out_ready, g + 1)
                sp.dma_start(ov[:, g * TG:(g + 1) * TG, :], x_all[:, g * TG:(g + 1) * TG, :]).then_inc(out_sent, 16)
            sp.wait_ge(out_sent, 16 * G)

        @block.gpsimd
        def _(pool):
            for e in range(E):
                last = nc.gpsimd.memset(rank[:, e:e + 1], float(E - e))
            last.then_inc(rank_ready, 1)
            nc.gpsimd.memset(pick_f[:], 1.0).then_inc(pick_ready, 1)
            pool.wait_ge(pick_ready, 1)
            for k in range(2):
                rows = slice(32 * k, 32 * k + 32)
                nc.gpsimd.affine_select(out=pick_f[rows, :, :], in_=pick_f[rows, :, :], compare_op=ALU.is_equal,
                                        fill=0.0, base=0, pattern=[[-1, E], [0, P]],
                                        channel_multiplier=1).then_inc(pick_ready, 1)

        @block.scalar
        def _(act):
            for g in range(G):
                act.wait_ge(turned, g + 1)
                nc.scalar.activation(xt[:, g * GT:(g + 1) * GT], ps[:, g, :], ACT.Copy).then_inc(xt_ready, 1)
            act.wait_ge(centred, 1)
            nc.scalar.activation(ex[:], lg[:], ACT.Exp).then_inc(exp_done, 1)
            for g in range(G):
                act.wait_ge(gates_turned, g + 1)
                nc.scalar.activation(gates_t[:, g * GT:(g + 1) * GT], ps[0:64, g, :], ACT.Copy)\
                  .then_inc(gates_t_ready, 1)
            act.sem_inc(gb_ready, 1)
            with act.Fori(0, G) as g:
                for k in range(K):
                    n = K * g + k
                    act.wait_ge(h_full, n + 1)
                    act.wait_ge(h_split, n + 1)
                    nc.scalar.activation(h[:, k % 2, :], ps[:, k % HR, :], ACT.Silu).then_inc(h_act, 1)
                    if k % FB == FB - 1:
                        e = k // FB
                        act.wait_ge(gb_full, E * g + e + 1)
                        act.wait_ge(y_used, E * g + e + 1)
                        nc.scalar.activation(gb[:, e % 2, :], ps[:, GB, :], ACT.Copy).then_inc(gb_ready, 1)

        @block.tensor
        def _(pe):
            def three(dst, w_hi, w_lo, x_hi, x_lo, start=True, stop=True):
                nc.tensor.matmul(dst, w_hi, x_hi, start=start, stop=False)
                nc.tensor.matmul(dst, w_hi, x_lo, start=False, stop=False)
                return nc.tensor.matmul(dst, w_lo, x_hi, start=False, stop=stop)

            for g in range(G):
                for t in range(TG):
                    mm = nc.tensor.transpose(ps[:, g, t * P:(t + 1) * P], u_all[:, g * TG + t, :], ident[:])
                mm.then_inc(turned, 1)
            for g in range(G):
                pe.wait_ge(xt_ready, g + 1)
                for t in range(g * TG, (g + 1) * TG):
                    mm = nc.tensor.matmul(ps[:, TR, t * E:(t + 1) * E], xt[:, t * P:(t + 1) * P], wr_sb[:],
                                          start=True, stop=True)
            mm.then_inc(logits_done, 1)
            pe.wait_ge(gates_ready, 1)
            for g in range(G):
                for t in range(TG):
                    mm = nc.tensor.transpose(ps[0:64, g, t * P:(t + 1) * P],
                                             gates[:, g * TG + t, :].bitcast(F32), ident[:])
                mm.then_inc(gates_turned, 1)
            pe.wait_ge(gates_t_ready, G)
            pe.wait_ge(xt_split, G)
            pe.wait_ge(pick_split, 1)
            pe.sem_inc(y_step, HR)
            with pe.Fori(0, G) as g:
                cols = bass.ds(g * GT, GT)

                def hidden(k):
                    e, f = divmod(k, FB)
                    three(ps[:, k % HR, :], ffn_w[0][:, e, f, :], ffn_w[1][:, e, f, :], xt_hi[:, cols],
                          xt_lo[:, cols]).then_inc(h_full, 1)
                    if f == 1:
                        pe.wait_ge(gb_ready, E * g + e + 1)
                        pe.sem_inc(gb_turn, 1)
                        nc.tensor.matmul(ps[:, GB, :], pick[:, e, :], gates_t[:, cols], start=True, stop=True)\
                          .then_inc(gb_full, 1)

                def back(k):
                    e, f = divmod(k, FB)
                    if f == 0:
                        pe.wait_ge(y_used, E * g + e + 1)
                    pe.wait_ge(h_split, 2 + K * g + k + 1)
                    three(ps[:, Y + e % 2, :], ffn_w[2][:, e, f, :], ffn_w[3][:, e, f, :], h_hi[:, k % HR, :],
                          h_lo[:, k % HR, :], start=(f == 0), stop=(f == FB - 1)).then_inc(y_step, 1)

                LAG = 2
                for k in range(K + LAG):
                    if k < K:
                        hidden(k)
                    if k >= LAG:
                        back(k - LAG)
                pe.wait_ge(acc_step, E * (g + 1))
                for t in range(TG):
                    mm = nc.tensor.transpose(ps[:, TR, t * P:(t + 1) * P], acc[:, t * P:(t + 1) * P], ident[:])
                mm.then_inc(acc_turned, 1)

        @block.vector
        def _(dve):
            step = [0]

            def chain(ins):
                step[0] += 1
                ins.then_inc(dve_step2, 1)
                dve.wait_ge(dve_step2, step[0])

            dve.wait_ge(rank_ready, 1)
            nc.vector.memset(gates[:].bitcast(F32), 0.0)
            dve.wait_ge(pick_ready, 3)
            nc.vector.tensor_copy(pick[:], pick_f[:]).then_inc(pick_split, 1)
            for g in range(G):
                cols = slice(g * GT, (g + 1) * GT)
                dve.wait_ge(xt_ready, g + 1)
                chain(nc.vector.tensor_copy(xt_hi[:, cols], xt[:, cols]))
                nc.vector.tensor_tensor(xt_lo[:, cols], xt[:, cols], xt_hi[:, cols].bitcast(F32), ALU.subtract)\
                  .then_inc(xt_split, 1)

            def wide(a):
                return a[:].unsqueeze(2).to_broadcast([P, NT, E])

            ranks = rank[:].unsqueeze(1).to_broadcast([P, NT, E])

            def largest(src, hot):
                chain(nc.vector.tensor_reduce(red[:], src, AX.X, ALU.max))
                chain(nc.vector.tensor_tensor(cand[:], src, wide(red), ALU.is_equal))
                chain(nc.vector.tensor_tensor(cand[:], cand[:], ranks, ALU.mult))
                chain(nc.vector.tensor_reduce(red[:], cand[:], AX.X, ALU.max))
                chain(nc.vector.tensor_tensor(hot[:], cand[:], wide(red), ALU.is_equal))

            dve.wait_ge(logits_done, 1)
            logits = ps[:, TR, 0:NT * E].rearrange("p (t e) -> p t e", e=E)
            chain(nc.vector.tensor_reduce(red[:], logits, AX.X, ALU.max))
            nc.vector.tensor_tensor(lg[:], logits, wide(red), ALU.subtract).then_inc(centred, 1)
            dve.wait_ge(centred, 1)
            largest(lg[:], first)
            chain(nc.vector.scalar_tensor_tensor(out=rest[:], in0=first[:], scalar=NEG, in1=lg[:], op0=ALU.mult,
                                                 op1=ALU.add))
            largest(rest[:], second)
            chain(nc.vector.tensor_tensor(first[:], first[:], second[:], ALU.add))
            dve.wait_ge(exp_done, 1)
            chain(nc.vector.tensor_tensor(first[:], first[:], ex[:], ALU.mult))
            chain(nc.vector.tensor_reduce(red[:], first[:], AX.X, ALU.add))
            chain(nc.vector.reciprocal(red[:], red[:]))
            chain(nc.vector.tensor_tensor(first[:], first[:], wide(red), ALU.mult))
            chain(nc.vector.tensor_copy(gates[:, :, 0:E], first[:]))
            nc.vector.tensor_tensor(gates[:, :, 32:32 + E], first[:], gates[:, :, 0:E].bitcast(F32),
                                    ALU.subtract).then_inc(gates_ready, 1)
            dve.sem_inc(h_split, 2)
            dve.sem_inc(y_used, 2)

            def gather(g, e):
                m = E * g + e
                dve.wait_ge(y_step, HR + FB * (m + 1))
                dve.wait_ge(gb_ready, 1 + m + 1)
                y = ps[:, Y + e % 2, :]
                if e == 0:
                    nc.vector.tensor_tensor(acc[:], y, gb[:, e % 2, :], ALU.mult).then_inc(y_used, 1)
                    dve.wait_ge(y_used, 2 + m + 1)
                    dve.sem_inc(acc_step, 1)
                else:
                    nc.vector.tensor_tensor(part[:], y, gb[:, e % 2, :], ALU.mult).then_inc(y_used, 1)
                    dve.wait_ge(y_used, 2 + m + 1)
                    nc.vector.tensor_tensor(acc[:], acc[:], part[:], ALU.add).then_inc(acc_step, 1)
                    dve.wait_ge(acc_step, m + 1)

            with dve.Fori(0, G) as g:
                for k in range(K):
                    n = K * g + k
                    dve.wait_ge(h_act, n + 1)
                    dve.wait_ge(y_step, n + 1)
                    nc.vector.tensor_copy(h_hi[:, k % HR, :], h[:, k % 2, :]).then_inc(h_hi_done, 1)
                    dve.wait_ge(h_hi_done, n + 1)
                    nc.vector.tensor_tensor(h_lo[:, k % HR, :], h[:, k % 2, :], h_hi[:, k % HR, :].bitcast(F32),
                                            ALU.subtract).then_inc(h_split, 1)
                    if k >= FB and k % FB == FB - 1:
                        gather(g, k // FB - 1)
                gather(g, E - 1)
                dve.wait_ge(acc_turned, g + 1)
                rows = bass.ds(g * TG, TG)
                nc.vector.tensor_tensor(x_all[:, rows, :], ps[:, TR, :].rearrange("p (t d) -> p t d", t=TG),
                                        x_all[:, rows, :], ALU.add).then_inc(out_ready, 1)


def kernel(**inputs):
    import numpy as np
    import concourse.bacc as bacc
    from concourse.bass_utils import run_bass_kernel_spmd

    a = {k.replace("L0_attn_", "").replace("L0_ffn_", ""): np.asarray(v) for k, v in inputs.items()}
    by_channel = lambda v: v.reshape(PAIRS, P).T
    arrays = {
        "x": a["x"].reshape(-1, D),
        "w_in": np.concatenate([a[n].T for n in ("WQ", "WK", "Wg", "WV")], axis=1),
        "w_out": a["WO"].T.reshape(PAIRS, P, D).transpose(1, 0, 2).reshape(P, CH),
        "b_in": np.stack([by_channel(a[n]) for n in ("bQ", "bK", "bg")], axis=1),
        "b_v": a["bV"].reshape(1, CH),
        "cols": np.stack([a["bO"], a["ln_gamma"], a["ln_beta"]], axis=1),
        "alpha": by_channel(a["alpha_logit"].reshape(-1)),
        "alpha_row": a["alpha_logit"].reshape(1, CH),
        "w1": a["W1"].transpose(2, 0, 1).reshape(D, E * DFF),
        "w2": a["W2"].reshape(E, D, FB, P).transpose(3, 0, 2, 1).reshape(P, E * DFF),
        "w_router": a["Wr"].T,
    }
    arrays = {f"in_{k}": np.ascontiguousarray(v) for k, v in arrays.items()}
    nc = bacc.Bacc("TRN2", target_bir_lowering=False, num_devices=1)
    args = [nc.dram_tensor(n, v.shape, mybir.dt.from_np(v.dtype), kind="ExternalInput").ap()
            for n, v in arrays.items()]
    out = nc.dram_tensor("out_0", arrays["in_x"].shape, F32, kind="ExternalOutput").ap()
    build(nc, *args, out)
    r = run_bass_kernel_spmd(nc, [arrays], core_ids=[0])
    return r.results[0]["out_0"].reshape(a["x"].shape)
```

```python
from contextlib import ExitStack

import concourse.bass as bass
from concourse import mybir

ALU = mybir.AluOpType
ACT = mybir.ActivationFunctionType
F32 = mybir.dt.float32
F32R = mybir.dt.float32r
I8 = mybir.dt.int8
I32 = mybir.dt.int32
AX = mybir.AxisListType

P = 128
SEQ = 256
D = 128
HEADS, DH = 16, 64
PAIRS = HEADS // 2
CH = HEADS * DH
E, DFF = 8, 512
FB = DFF // P
EPS = 1e-5
GT = 512
LOGIT_MIN = -3.5
LEVELS = [16, 8, 4, 2, 1]
MID, S32, S64, S128 = 0, SEQ, SEQ + SEQ // 2, 2 * SEQ
VER = 5 * SEQ // 2
NEG = -3.0e38


def build(nc, x, w_in, w_out, b_in, b_v, cols, alpha, alpha_row, w1, w2, w_router, out):
    T = x.shape[0]
    NT = T // P
    G = T // GT
    TG = GT // P
    NB = GT // SEQ

    outer = ExitStack()
    with outer:
        def sb(name, shape, dt=F32, ctx=outer):
            return ctx.enter_context(nc.sbuf_tensor(name, shape, dt))

        def sem(name, ctx=outer):
            return ctx.enter_context(nc.semaphore(name))

        x_all = sb("x_all", [P, NT, D])
        u_all = sb("u_all", [P, NT, D])
        ident = sb("ident", [P, P])
        w1_hi = sb("w1_hi", [P, E, FB, P], F32R)
        w1_lo = sb("w1_lo", [P, E, FB, P], F32R)
        w2_hi = sb("w2_hi", [P, E, FB, P], F32R)
        w2_lo = sb("w2_lo", [P, E, FB, P], F32R)
        wr_sb = sb("wr_sb", [P, E])
        ffn_split = sem("ffn_split")
        ident_ready = sem("ident_ready")

        attention(nc, sb, sem, x, w_in, w_out, b_in, b_v, cols, alpha, alpha_row, w1, w2, w_router,
                  x_all, u_all, ident, ident_ready,
                  (w1_hi, w1_lo, w2_hi, w2_lo), wr_sb, ffn_split, NT, G, TG, NB)
        experts(nc, sb, sem, out, x_all, u_all, ident,
                (w1_hi, w1_lo, w2_hi, w2_lo), wr_sb, NT, G, TG)


def attention(nc, sb_, sem_, x, w_in, w_out, b_in, b_v, cols, alpha, alpha_row, w1, w2, w_router,
              x_all, u_all, ident, ident_ready, ffn_w, wr_sb,
              ffn_split, NT, G, TG, NB):
    ctx = ExitStack()
    with ctx:
        def sb(name, shape, dt=F32):
            return sb_(name, shape, dt, ctx)

        def sem(name):
            return sem_(name, ctx)

        wi_hi = sb("wi_hi", [P, 4, CH], F32R)
        wi_lo = sb("wi_lo", [P, 4, CH], F32R)
        wo_hi = sb("wo_hi", [P, PAIRS, D], F32R)
        wo_lo = sb("wo_lo", [P, PAIRS, D], F32R)
        STG, CHUNK = 2, 512
        stage = sb("stage", [P, STG, CHUNK])
        bi = sb("bi", [P, 3, PAIRS])
        bv = sb("bv", [P, CH])
        col = sb("col", [P, 3])
        al = sb("al", [P, PAIRS])
        al_min = sb("al_min", [1, 1])
        narrow = sb("narrow", [1, 1], I32)
        pow_up = sb("pow_up", [P, PAIRS, 129])
        pow_dn = sb("pow_dn", [P, PAIRS, 129])
        mid_q = sb("mid_q", [P, PAIRS, 32])
        mid_k = sb("mid_k", [P, PAIRS, 32])
        mask = sb("mask", [P, 1 + len(LEVELS), 3, P], I8)
        xn = sb("xn", [P, GT])
        xn_hi = sb("xn_hi", [P, GT], F32R)
        xn_lo = sb("xn_lo", [P, GT], F32R)
        v_sb = sb("v_sb", [P, TG, CH])
        q_raw = sb("q_raw", [P, GT])
        k_raw = sb("k_raw", [P, GT])
        gate = sb("gate", [P, 2, GT])
        qv = sb("qv", [P, 2, NB, VER])
        kv = sb("kv", [P, 2, NB, VER])
        a_sb = sb("a_sb", [P, NB, 2, 3 * P])
        og = sb("og", [P, GT])
        z = sb("z", [P, TG, D])
        stats = sb("stats", [P, TG, 6])
        mv = sb("mv", [P, TG, 2])
        std = sb("std", [P, TG])
        rstd = sb("rstd", [P, TG])
        shift = sb("shift", [P, TG])
        mv3 = sb("mv3", [P, TG, 2])
        std3 = sb("std3", [P, TG])
        rstd3 = sb("rstd3", [P, TG])
        shift3 = sb("shift3", [P, TG])
        eps_col = sb("eps_col", [P, 1])
        og_hi = sb("og_hi", [P, GT], F32R)
        og_lo = sb("og_lo", [P, GT], F32R)
        y_sb = sb("y_sb", [P, GT])

        al_row = v_sb[0:1, TG - 1, :]
        causal = og[:, 0:3 * P].rearrange("p (t q) -> p t q", t=3)
        it = y_sb[:, 0:2 * P].bitcast(I32).rearrange("p (a q) -> p a q", a=2)
        ring = ctx.enter_context(nc.psum_tensor("ring", [P, 2, 512], F32))
        sc = ctx.enter_context(nc.psum_tensor("sc", [P, NB, 2, 512], F32))
        ps_o = ctx.enter_context(nc.psum_tensor("ps_o", [P, 512], F32))
        ps_y = ctx.enter_context(nc.psum_tensor("ps_y", [P, 512], F32))

        x0_in = sem("x0_in")
        x_loaded = sem("x_loaded")
        small_in = sem("small_in")
        al_in = sem("al_in")
        hi_done = sem("hi_done")
        lo_done = sem("lo_done")
        stats_done = sem("stats_done")
        std_done = sem("std_done")
        stats3_done = sem("stats3_done")
        std3_done = sem("std3_done")
        zeros_ready = sem("zeros_ready")
        norm_turn = sem("norm_turn")
        sig_done = sem("sig_done")
        dve_step = sem("dve_step")
        mask_ready = sem("mask_ready")
        narrow_ready = sem("narrow_ready")
        z_ready = sem("z_ready")
        u_step = sem("u_step")
        xn_raw = sem("xn_raw")
        xn_ready = sem("xn_ready")
        v_ready = sem("v_ready")
        ring_full = [sem(f"ring_full{r}") for r in range(2)]
        raw_ready = sem("raw_ready")
        ver_ready = sem("ver_ready")
        gate_ready = sem("gate_ready")
        sc_done = sem("sc_done")
        keep_turn = sem("keep_turn")
        a_ready = sem("a_ready")
        out_done = sem("out_done")
        o_read = sem("o_read")
        og_raw = sem("og_raw")
        og_ready = sem("og_ready")
        wo_done = sem("wo_done")
        y_ready = sem("y_ready")
        lv_ready = sem("lv_ready")
        scale_ready = sem("scale_ready")
        scale3_ready = sem("scale3_ready")
        scale_turn = sem("scale_turn")
        eps_ready = sem("eps_ready")
        u_ready = sem("u_ready")
        u3_ready = sem("u3_ready")
        iota_ready = sem("iota_ready")
        y_read = sem("y_read")
        stage_in = [sem(f"stage_in{i}") for i in range(STG)]

        wi_h, wi_l = [w[:].rearrange("p a c -> p (a c)") for w in (wi_hi, wi_lo)]
        wo_h, wo_l = [w[:].rearrange("p a c -> p (a c)") for w in (wo_hi, wo_lo)]
        f_h = [w[:].rearrange("p e b c -> p (e b c)") for w in (ffn_w[0], ffn_w[2])]
        f_l = [w[:].rearrange("p e b c -> p (e b c)") for w in (ffn_w[1], ffn_w[3])]
        chunks = [(w_in, wi_h, wi_l, j * CH) for j in (3, 0, 1, 2)]
        chunks += [(w_out, wo_h, wo_l, c) for c in range(0, CH, CHUNK)]
        chunks += [(w_in, wi_h, wi_l, j * CH + CHUNK) for j in (3, 0, 1, 2)]
        FIRST = len(chunks)
        for i, src in enumerate((w1, w2)):
            chunks += [(src, f_h[i], f_l[i], c * CHUNK) for c in range(E * DFF // CHUNK)]
        lands = [(t[:, 0], half) for t in (qv, kv) for half in range(2)] + [None] * (CH // CHUNK)
        lands += [(t[:, 1], half) for t in (qv, kv) for half in range(2)]
        lands += [None] * (len(chunks) - FIRST)
        staged, landing, arrival = [], [], []
        for n in range(len(chunks)):
            if lands[n]:
                t, half = lands[n]
                landing.append(t.rearrange("p b v -> p (b v)")[:, half * CHUNK:(half + 1) * CHUNK])
                arrival.append((sem(f"chunk_in{n}"), 16))
            else:
                landing.append(stage[:, len(staged) % STG, :])
                arrival.append((stage_in[len(staged) % STG], 16 * (len(staged) // STG + 1)))
                staged.append(n)

        start_uses = [("turn_z", 0)] + [("v", t) for t in range(TG)] + [("proj", 0, j) for j in range(3)]
        body_uses = []
        for p in range(PAIRS - 1):
            body_uses += [("proj", p + 1, j) for j in range(3)]
            if p < TG:
                body_uses.insert(len(body_uses) - (p == 0), ("v", TG + p))
        LAST_USES = len(body_uses) + 1
        ahead = len(body_uses)
        body_uses += start_uses + [("turn_y",)]
        assert len(start_uses) % 2 == 0 and len(body_uses) % 2 == 0

        def use_of(kind, own=True):
            if not own:
                return ahead + start_uses.index(kind)
            return LAST_USES - 1 if kind == ("last_y",) else body_uses.index(kind)

        def full_at(i, g):
            return i // 2 + 1 if g is None else len(start_uses) // 2 + g * (len(body_uses) // 2) + i // 2 + 1

        def read_by(kind, g):
            if kind[0] == "turn_z":
                return xn_raw, g + 1
            if kind[0] == "v":
                return v_ready, 2 * TG * g + kind[1] + 1
            if kind[0] == "turn_y":
                return y_read, 1 + g + 1
            _, p, j = kind
            return (raw_ready, 2 * (PAIRS * g + p) + j + 1) if j < 2 else (gate_ready, PAIRS * g + p + 1)

        block = ctx.enter_context(nc.Block())

        @block.sync
        def _(sp):
            xv = x.rearrange("(t p) d -> p t d", p=P)

            def rows_in(g):
                sp.dma_start(x_all[:, g * TG:(g + 1) * TG, :], xv[:, g * TG:(g + 1) * TG, :])\
                  .then_inc(x0_in if g == 0 else x_loaded, 16)

            rows_in(0)
            small = [(col[:], cols), (bi[:], b_in), (bv[:], b_v.to_broadcast([P, CH])), (al_row, alpha_row),
                     (wr_sb[:], w_router)]
            for n, (src, _, _, c) in enumerate(chunks):
                if n == FIRST:
                    for g in range(1, G):
                        rows_in(g)
                if n in staged and staged.index(n) >= STG:
                    sp.wait_ge(lo_done, staged[staged.index(n) - STG] + 1)
                sp.dma_start(landing[n], src[:, c:c + CHUNK]).then_inc(arrival[n][0], 16)
                if n < len(small):
                    sp.dma_start(*small[n]).then_inc(small_in, 16)

        @block.gpsimd
        def _(pool):
            nc.gpsimd.memset(ident[:], 1.0).then_inc(mask_ready, 1)
            nc.gpsimd.memset(causal, 1.0).then_inc(mask_ready, 1)
            pool.wait_ge(mask_ready, 2)
            nc.gpsimd.affine_select(out=ident[:], in_=ident[:], compare_op=ALU.is_equal, fill=0.0, base=0,
                                    pattern=[[1, P]], channel_multiplier=-1).then_inc(ident_ready, 1)
            for t in (0, 2):
                nc.gpsimd.affine_select(out=causal[:, t, :], in_=causal[:, t, :], compare_op=ALU.is_ge, fill=0.0,
                                        base=0, pattern=[[1, P]], channel_multiplier=-1).then_inc(mask_ready, 1)
            nc.gpsimd.iota(it[:, 0, :], pattern=[[1, P]], base=0, channel_multiplier=0).then_inc(iota_ready, 1)
            nc.gpsimd.iota(it[:, 1, :], pattern=[[0, P]], base=0, channel_multiplier=1).then_inc(iota_ready, 1)
            nc.gpsimd.memset(a_sb[:], 0.0).then_inc(zeros_ready, 1)
            for n, (_, hi, lo, c) in enumerate(chunks):
                h, l = hi[:, c:c + CHUNK], lo[:, c:c + CHUNK]
                if n < FIRST:
                    pool.wait_ge(hi_done, n + 1)
                else:
                    pool.wait_ge(*arrival[n])
                    nc.gpsimd.tensor_copy(h, landing[n]).then_inc(ffn_split, 1)
                    pool.wait_ge(ffn_split, n - FIRST + 1)
                nc.gpsimd.tensor_tensor(l, landing[n], h.bitcast(F32), ALU.subtract).then_inc(lo_done, 1)

        @block.scalar
        def _(act):
            act.dma_start(al[:], alpha).then_inc(al_in, 16)

            def high(n):
                _, hi, _, c = chunks[n]
                act.wait_ge(*arrival[n])
                nc.scalar.activation(hi[:, c:c + CHUNK], landing[n], ACT.Copy).then_inc(hi_done, 1)

            def deviations(g, which):
                act.wait_ge(stats_done, 2 * g + which + 1)
                nc.scalar.activation(std[:], mv[:, :, 1], ACT.Sqrt, bias=eps_col[:, 0:1])\
                  .then_inc(std_done, 1)

            def rows_of(buf, g, t):
                return buf[:, bass.ds(g * TG + t, 1), :].rearrange("p a d -> p (a d)")

            def normalised(dst, src, g, rstd_, shift_):
                act.sem_inc(scale_turn, 1)
                for t in range(TG):
                    last = nc.scalar.activation(dst(t), rows_of(src, g, t), ACT.Identity, bias=shift_[:, t:t + 1],
                                                scale=rstd_[:, t:t + 1])
                return last

            def write_u(g):
                act.wait_ge(scale_ready, 2 * g + 1)
                normalised(lambda t: rows_of(u_all, g, t), x_all, g, rstd, shift).then_inc(u_ready, 1)

            def write_z(g):
                act.wait_ge(scale_ready, 2 * g + 2)
                normalised(lambda t: z[:, t, :], u_all, g, rstd, shift).then_inc(z_ready, 1)

            def filled(i, g):
                act.wait_ge(ring_full[i % 2], full_at(i, g))
                return ring[:, i % 2, :]

            def xn_out(g, i, at):
                src = filled(i, at)
                nc.scalar.activation(xn_hi[:], src, ACT.Identity, bias=col[:, 2:3], scale=col[:, 1:2])
                nc.scalar.activation(xn[:], src, ACT.Identity, bias=col[:, 2:3], scale=col[:, 1:2])\
                  .then_inc(xn_raw, 1)

            def evac_qk(p, g, uses, at):
                for j, dst in enumerate((q_raw, k_raw)):
                    src = filled(uses[j], at)
                    act.wait_ge(ver_ready, 2 * (PAIRS * g + p) + j + 1)
                    nc.scalar.activation(dst[:], src, ACT.Identity, bias=bi[:, j, p:p + 1]).then_inc(raw_ready, 1)

            def evac_gate(p, g, uses, at):
                src = filled(uses[2], at)
                act.wait_ge(og_ready, PAIRS * g + p + 1)
                nc.scalar.activation(gate[:, p % 2, :], src, ACT.Silu, bias=bi[:, 2, p:p + 1])\
                  .then_inc(gate_ready, 1)

            def uses_of(p, own=True):
                return [use_of(("proj", p, j), own) for j in range(3)]

            act.wait_ge(eps_ready, 1)
            nc.scalar.activation(std3[:, 0:1], eps_col[:, 0:1], ACT.Sqrt)
            deviations(0, 0)
            write_u(0)
            high(0)
            deviations(0, 1)
            write_z(0)
            act.wait_ge(al_in, 16)
            nc.scalar.activation(pow_up[:, :, 1], al[:], ACT.Sigmoid).then_inc(sig_done, 1)
            for n in range(1, 4):
                high(n)
            act.wait_ge(small_in, 5 * 16)
            xn_out(0, 0, None)
            for n in range(4, FIRST):
                high(n)
            first_uses = [start_uses.index(("proj", 0, j)) for j in range(3)]
            evac_qk(0, 0, first_uses, None)
            evac_gate(0, 0, first_uses, None)
            evac_qk(1, 0, uses_of(1), 0)
            evac_gate(1, 0, uses_of(1), 0)
            evac_qk(2, 0, uses_of(2), 0)
            evac_gate(2, 0, uses_of(2), 0)

            def body(g, last):
                for p in range(3, PAIRS):
                    evac_qk(p, g, uses_of(p), g)
                    evac_gate(p, g, uses_of(p), g)
                    if not last and p in (3, 5):
                        deviations(g + 1, (p - 3) // 2)
                    if not last and p == 4:
                        write_u(g + 1)
                    if not last and p == 6:
                        write_z(g + 1)
                if not last:
                    xn_out(g + 1, use_of(("turn_z", 0), False), g)
                    ahead_uses = uses_of(0, False)
                    evac_qk(0, g + 1, ahead_uses, g)
                act.wait_ge(wo_done, 1 + PAIRS * g + PAIRS)
                nc.scalar.activation(y_sb[:], ps_y[:], ACT.Identity, bias=col[:, 0:1]).then_inc(y_ready, 1)
                if not last:
                    evac_gate(0, g + 1, ahead_uses, g)
                    evac_qk(1, g + 1, uses_of(1), g + 1)
                    evac_gate(1, g + 1, uses_of(1), g + 1)
                    evac_qk(2, g + 1, uses_of(2), g + 1)
                act.wait_ge(stats3_done, g + 1)
                nc.scalar.activation(std3[:], mv3[:, :, 1], ACT.Sqrt, bias=eps_col[:, 0:1]).then_inc(std3_done, 1)
                if not last:
                    evac_gate(2, g + 1, uses_of(2), g + 1)
                act.wait_ge(scale3_ready, g + 1)
                normalised(lambda t: rows_of(u_all, g, t), x_all, g, rstd3, shift3).then_inc(u3_ready, 1)

            with act.Fori(0, G - 1) as g:
                body(g, False)
            body(G - 1, True)

        @block.tensor
        def _(pe):
            def three(dst, w_hi, w_lo, x_hi, x_lo, start=True, stop=True):
                nc.tensor.matmul(dst, w_hi, x_hi, start=start, stop=False)
                nc.tensor.matmul(dst, w_hi, x_lo, start=False, stop=False)
                return nc.tensor.matmul(dst, w_lo, x_hi, start=False, stop=stop)

            def at(i, before=None):
                if before:
                    pe.wait_ge(*before)
                return ring[:, i % 2, :], ring_full[i % 2]

            def turn(dst, full, src):
                for t in range(TG):
                    mm = nc.tensor.transpose(dst[:, t * P:(t + 1) * P], src[:, t * P:(t + 1) * P], ident[:])
                mm.then_inc(full, 1)

            def value(use, bank):
                dst, full = bank
                h, t = divmod(use, TG)
                rows, c = slice(t * P, (t + 1) * P), slice(h * 512, (h + 1) * 512)
                three(dst, xn_hi[:, rows], xn_lo[:, rows], wi_hi[:, 3, c], wi_lo[:, 3, c]).then_inc(full, 1)

            def proj(p, j, bank):
                dst, full = bank
                c = slice(p * P, (p + 1) * P)
                three(dst, wi_hi[:, j, c], wi_lo[:, j, c], xn_hi[:], xn_lo[:]).then_inc(full, 1)

            z_flat = z[:].rearrange("p t d -> p (t d)")

            def body(g, last, levels):
                R = 1 + len(levels)

                def claim(kind, own=True):
                    i = use_of(kind, own)
                    if i == 0:
                        before = gate_ready, PAIRS * g + 1
                    elif i == 1:
                        before = y_read, g + 1
                    else:
                        before = read_by(body_uses[i - 2], g + 1 if i - 2 >= ahead else g)
                    return at(i, before)

                def diagonal(p, b, r, c0):
                    h = slice(r * DH, (r + 1) * DH)
                    for t in range(2):
                        mm = nc.tensor.matmul(sc[:, b, r, 2 * t * P:2 * t * P + P],
                                              kv[h, p % 2, b, c0 + t * P:c0 + (t + 1) * P],
                                              qv[h, p % 2, b, c0 + t * P:c0 + (t + 1) * P],
                                              start=True, stop=True)
                    return mm

                def scores(p, b):
                    n = PAIRS * g + p
                    pe.wait_ge(ver_ready, 2 + 2 * n + 2)
                    pe.wait_ge(a_ready, 2 * R * n + b + 1)
                    for r in range(2):
                        diagonal(p, b, r, MID)
                    for r in range(2):
                        h = slice(r * DH, (r + 1) * DH)
                        for t in range(2):
                            for L, c in ((32, S32), (64, S64)):
                                for i in range(64 // L):
                                    s0 = c + 64 * t + i * L
                                    key = 2 * L * i
                                    q0 = 2 * t * P + key + L
                                    nc.tensor.matmul(sc[key:key + L, b, r, q0:q0 + L], kv[h, p % 2, b, s0:s0 + L],
                                                     qv[h, p % 2, b, s0:s0 + L], start=True, stop=True)
                        mm = nc.tensor.matmul(sc[:, b, r, P:2 * P], kv[h, p % 2, b, S128:S128 + P],
                                              qv[h, p % 2, b, S128:S128 + P], start=True, stop=True)
                    mm.then_inc(sc_done, 1)

                def finer(p):
                    n = PAIRS * g + p
                    for i, L in enumerate(levels):
                        pe.wait_ge(lv_ready, len(levels) * n + i + 1)
                        for b in range(NB):
                            pe.wait_ge(a_ready, 2 * R * n + 2 * (i + 1) + b + 1)
                            for r in range(2):
                                mm = diagonal(p, b, r, S32)
                            mm.then_inc(sc_done, 1)

                def outs(p):
                    n = PAIRS * g + p
                    if p == 0:
                        pe.wait_ge(v_ready, 2 * TG * g + TG)
                    if p == PAIRS // 2:
                        pe.wait_ge(v_ready, 2 * TG * g + 2 * TG)
                    pe.wait_ge(o_read, n + 1)
                    for b in range(NB):
                        pe.wait_ge(a_ready, 2 + 2 * R * n + 2 * (R - 1) + b + 1)
                        dst = ps_o[:, b * SEQ:(b + 1) * SEQ]
                        c = [slice(p * P + r * DH, p * P + (r + 1) * DH) for r in range(2)]
                        for r in range(2):
                            nc.tensor.matmul(dst[r * DH:(r + 1) * DH, :], v_sb[:, 2 * b, c[r]],
                                             a_sb[:, b, r, 0:2 * P], start=True, stop=False,
                                             skip_group_check=True)
                        for r in range(2):
                            mm = nc.tensor.matmul(dst[r * DH:(r + 1) * DH, P:2 * P], v_sb[:, 2 * b + 1, c[r]],
                                                  a_sb[:, b, r, 2 * P:3 * P], start=False, stop=True,
                                                  skip_group_check=True)
                        mm.then_inc(out_done, 1)

                def project_out(p):
                    n = PAIRS * g + p
                    pe.wait_ge(og_ready, 2 + n + 1)
                    three(ps_y[:], wo_hi[:, p, :], wo_lo[:, p, :], og_hi[:], og_lo[:], start=(p == 0),
                          stop=(p == PAIRS - 1)).then_inc(wo_done, 1)

                for p in range(PAIRS):
                    if p + 1 < PAIRS:
                        for j in range(2):
                            proj(p + 1, j, claim(("proj", p + 1, j)))
                    if p == 0:
                        pe.wait_ge(lo_done, FIRST)
                        value(TG, claim(("v", TG)))
                    scores(p, 0)
                    if p + 1 < PAIRS:
                        proj(p + 1, 2, claim(("proj", p + 1, 2)))
                    scores(p, 1)
                    finer(p)
                    if 0 < p < TG:
                        value(TG + p, claim(("v", TG + p)))
                    if p == PAIRS - 1 and not last:
                        pe.wait_ge(xn_ready, g + 2)
                        for t in range(TG // 2):
                            value(t, claim(("v", t), False))
                    if p:
                        project_out(p - 1)
                    if p == PAIRS - 1 and not last:
                        for t in range(TG // 2, TG):
                            value(t, claim(("v", t), False))
                    outs(p)
                    if p == PAIRS - 2 and not last:
                        bank = claim(("turn_z", 0), False)
                        pe.wait_ge(z_ready, g + 2)
                        turn(*bank, z_flat)
                if not last:
                    for j in range(2):
                        proj(0, j, claim(("proj", 0, j), False))
                project_out(PAIRS - 1)
                if not last:
                    proj(0, 2, claim(("proj", 0, 2), False))
                bank = claim(("last_y",) if last else ("turn_y",))
                pe.wait_ge(y_ready, g + 1)
                turn(*bank, y_sb)

            def groups(levels):
                pe.sem_inc(sc_done, 2 * (1 + len(levels)) + 1)
                with pe.Fori(0, G - 1) as g:
                    body(g, False, levels)
                body(G - 1, True, levels)

            def start_claim(i):
                return at(i, read_by(start_uses[i - 2], 0) if i >= 2 else None)

            pe.wait_ge(ident_ready, 1)
            pe.wait_ge(z_ready, 1)
            turn(*start_claim(0), z_flat)
            pe.wait_ge(xn_ready, 1)
            pe.wait_ge(lo_done, 1)
            for t in range(TG):
                value(t, start_claim(1 + t))
            for j in range(3):
                pe.wait_ge(lo_done, 2 + j)
                proj(0, j, start_claim(1 + TG + j))
            pe.sem_inc(out_done, 2)
            pe.sem_inc(wo_done, 1)
            pe.wait_ge(narrow_ready, 1)
            small_logit = pe.value_load(narrow[0:1, 0:1], min_val=0, max_val=1)
            with pe.If(small_logit):
                groups(LEVELS)
            with pe.Else():
                groups([])

        @block.vector
        def _(dve):
            step = [0]

            def chain(ins):
                step[0] += 1
                ins.then_inc(dve_step, 1)
                dve.wait_ge(dve_step, step[0])

            def rows_of(buf, g, t):
                return buf[:, bass.ds(g * TG + t, 1), :].rearrange("p a d -> p (a d)")

            def moments(src, g, mv_, link):
                dve.sem_inc(norm_turn, 1)
                for t in range(TG):
                    last = nc.vector.bn_stats(stats[:, t, :], rows_of(src, g, t))
                link(last)
                dve.sem_inc(norm_turn, 1)
                for t in range(TG):
                    last = nc.vector.bn_aggr(mv_[:, t, :], stats[:, t, :])
                return last

            def scales(mv_, std_, rstd_, shift_, link):
                link(nc.vector.reciprocal(rstd_[:], std_[:]))
                return nc.vector.scalar_tensor_tensor(out=shift_[:], in0=mv_[:, :, 0], scalar=-1.0, in1=rstd_[:],
                                                      op0=ALU.mult, op1=ALU.mult)

            def rows_a(g, link):
                if link is not chain:
                    dve.wait_ge(z_ready, g)
                moments(x_all, g, mv, link).then_inc(stats_done, 1)

            def rows_b(g, link):
                dve.wait_ge(std_done, 2 * g + 1)
                scales(mv, std, rstd, shift, link).then_inc(scale_ready, 1)

            def rows_c(g, link):
                dve.wait_ge(u_ready, g + 1)
                moments(u_all, g, mv, link).then_inc(stats_done, 1)

            def rows_d(g, link):
                r = bass.ds(g * TG, TG)
                link(nc.vector.tensor_tensor(x_all[:, r, :], x_all[:, r, :], u_all[:, r, :], ALU.add))
                dve.wait_ge(std_done, 2 * g + 2)
                scales(mv, std, rstd, shift, link).then_inc(scale_ready, 1)

            def split_xn(g):
                dve.wait_ge(xn_raw, g + 1)
                nc.vector.tensor_tensor(xn_lo[:], xn[:], xn_hi[:].bitcast(F32), ALU.subtract).then_inc(xn_ready, 1)

            def filled(i, g):
                dve.wait_ge(ring_full[i % 2], full_at(i, g))
                return ring[:, i % 2, :]

            def value_out(use, src):
                h, t = divmod(use, TG)
                c = slice(h * 512, (h + 1) * 512)
                nc.vector.tensor_tensor(v_sb[:, t, c], src, bv[:, c], ALU.add).then_inc(v_ready, 1)

            def doubled(ks):
                for k in ks:
                    a_k = pow_up[:, :, k:k + 1].to_broadcast([P, PAIRS, k])
                    nc.vector.tensor_tensor(pow_up[:, :, k + 1:2 * k + 1], pow_up[:, :, 1:k + 1], a_k, ALU.mult)
                    chain(nc.vector.tensor_tensor(pow_dn[:, :, 128 - 2 * k:128 - k], pow_dn[:, :, 128 - k:128],
                                                  a_k, ALU.mult))

            dve.sem_inc(ver_ready, 2)
            dve.sem_inc(a_ready, 2)
            dve.sem_inc(o_read, 1)
            dve.sem_inc(y_read, 1)
            dve.sem_inc(og_ready, 2)
            nc.vector.memset(eps_col[:], EPS).then_inc(eps_ready, 1)
            nc.vector.memset(pow_up[:, :, 0], 1.0)
            chain(nc.vector.memset(pow_dn[:, :, 128], 1.0))
            dve.wait_ge(x0_in, 16)
            rows_a(0, chain)
            rows_b(0, chain)
            rows_c(0, chain)
            rows_d(0, chain)
            dve.wait_ge(sig_done, 1)
            chain(nc.vector.tensor_copy(pow_dn[:, :, 127], pow_up[:, :, 1]))
            doubled([1, 2, 4, 8])
            nc.vector.tensor_copy(mid_q[:, :, 16:32], pow_up[:, :, 0:16])
            nc.vector.tensor_copy(mid_k[:, :, 0:16], pow_dn[:, :, 112:128])
            split_xn(0)
            nc.vector.reciprocal(mid_q[:, :, 0:16], pow_dn[:, :, 112:128])
            nc.vector.reciprocal(mid_k[:, :, 16:32], pow_up[:, :, 0:16])
            for t in range(TG):
                value_out(t, filled(1 + t, None))
                if t == 0:
                    dve.wait_ge(small_in, 5 * 16)
                    chain(nc.vector.tensor_reduce(al_min[:], al_row, AX.X, ALU.min))
                    nc.vector.tensor_scalar(narrow[:], al_min[:], LOGIT_MIN, None, ALU.is_lt)\
                      .then_inc(narrow_ready, 1)
            doubled([16, 32, 64])
            dve.wait_ge(mask_ready, 4)
            dve.wait_ge(zeros_ready, 1)

            def groups(levels):
                R = 1 + len(levels)

                def decayed(dst, raw, p, odd, tab_mid, tab):
                    def spans(L):
                        return raw[:].rearrange("c (b n o l) -> c b n o l", b=NB, o=2, l=L)[:, :, :, odd, :]

                    if R == 1:
                        nc.vector.tensor_tensor(
                            dst[:, p % 2, :, MID:S32].rearrange("c b (n l) -> c b n l", l=32),
                            raw[:].rearrange("c (b n l) -> c b n l", b=NB, l=32),
                            tab_mid[:, p:p + 1, :].unsqueeze(1).to_broadcast([P, NB, SEQ // 32, 32]),
                            ALU.mult)
                    else:
                        nc.vector.tensor_copy(dst[:, p % 2, :, MID:S32],
                                              raw[:].rearrange("c (b n) -> c b n", b=NB))
                    for L, c in ((32, S32), (64, S64), (128, S128)):
                        n = SEQ // (2 * L)
                        last = nc.vector.tensor_tensor(
                            dst[:, p % 2, :, c:c + P].rearrange("c b (n l) -> c b n l", l=L), spans(L),
                            tab(p, L).unsqueeze(1).to_broadcast([P, NB, n, L]), ALU.mult)
                    return last

                def up(p, L):
                    return pow_up[:, p:p + 1, 0:L]

                def down(p, L):
                    return pow_dn[:, p:p + 1, P - L:P]

                def versions_q(p, g):
                    n = PAIRS * g + p
                    dve.wait_ge(sc_done, 2 * R * n + 1)
                    dve.wait_ge(raw_ready, 2 * n + 1)
                    decayed(qv, q_raw, p, 1, mid_q, up).then_inc(ver_ready, 1)

                def versions_k(p, g):
                    n = PAIRS * g + p
                    dve.wait_ge(raw_ready, 2 * n + 2)
                    decayed(kv, k_raw, p, 0, mid_k, down).then_inc(ver_ready, 1)

                def versions(p, g):
                    versions_q(p, g)
                    versions_k(p, g)

                def keep(b, i):
                    m = mask[:, i, :, :].rearrange("p t q -> p (t q)").unsqueeze(1)
                    dve.sem_inc(keep_turn, 1)
                    nc.vector.copy_predicated(a_sb[:, b, :, :], m.to_broadcast([P, 2, 3 * P]),
                                              sc[:, b, :, 0:3 * P]).then_inc(a_ready, 1)

                def level(dst, p, tab, L):
                    return nc.vector.tensor_tensor(
                        dst[:, p % 2, :, S32:S32 + SEQ].rearrange("c b (n l) -> c b n l", l=L),
                        dst[:, p % 2, :, MID:MID + SEQ].rearrange("c b (n l) -> c b n l", l=L),
                        tab(p, L).unsqueeze(1).to_broadcast([P, NB, SEQ // L, L]), ALU.mult)

                def masked(p, g):
                    n = PAIRS * g + p
                    for b in range(NB):
                        dve.wait_ge(sc_done, 2 * R + 1 + 2 * R * n + b + 1)
                        dve.wait_ge(out_done, 2 * n + b + 1)
                        keep(b, 0)
                    for i, L in enumerate(levels):
                        level(qv, p, up, L)
                        level(kv, p, down, L).then_inc(lv_ready, 1)
                        for b in range(NB):
                            dve.wait_ge(sc_done, 2 * R + 1 + 2 * R * n + 2 * (i + 1) + b + 1)
                            keep(b, 1 + i)

                def gated(p, g):
                    n = PAIRS * g + p
                    dve.wait_ge(out_done, 2 + 2 * n + 2)
                    dve.wait_ge(gate_ready, n + 1)
                    nc.vector.tensor_tensor(og[:], ps_o[:], gate[:, p % 2, :], ALU.mult).then_inc(o_read, 1)
                    dve.wait_ge(o_read, 1 + n + 1)
                    dve.wait_ge(wo_done, n + 1)
                    nc.vector.tensor_copy(og_hi[:], og[:]).then_inc(og_raw, 1)
                    dve.wait_ge(og_raw, n + 1)
                    nc.vector.tensor_tensor(og_lo[:], og[:], og_hi[:].bitcast(F32), ALU.subtract)\
                      .then_inc(og_ready, 1)

                def first_scores(g):
                    versions_k(0, g)
                    dve.wait_ge(lo_done, FIRST)
                    versions(1, g)
                    masked(0, g)
                    value_out(TG, filled(use_of(("v", TG)), g))

                STEPS = 7

                def body(g, last):
                    done = [0]

                    def link(ins):
                        done[0] += 1
                        ins.then_inc(u_step, 1)
                        dve.wait_ge(u_step, STEPS * g + done[0])

                    for p in range(1, PAIRS):
                        if 2 <= p < PAIRS - 1:
                            versions(p + 1, g)
                        if not last and p in (2, 3, 4, 5):
                            if p == 2:
                                dve.wait_ge(x_loaded, 16 * (G - 1))
                            (rows_a, rows_b, rows_c, rows_d)[p - 2](g + 1, link)
                        masked(p, g)
                        if p < TG:
                            value_out(TG + p, filled(use_of(("v", TG + p)), g))
                        if p == PAIRS - 1 and not last:
                            for t in range(TG):
                                value_out(t, filled(use_of(("v", t), False), g))
                        gated(p, g)
                        if p == PAIRS - 2 and not last:
                            split_xn(g + 1)
                    if not last:
                        versions_q(0, g + 1)
                    src = filled(use_of(("last_y",) if last else ("turn_y",)), g)
                    r = bass.ds(g * TG, TG)
                    nc.vector.tensor_tensor(x_all[:, r, :], src.rearrange("p (t d) -> p t d", t=TG),
                                            x_all[:, r, :], ALU.add).then_inc(y_read, 1)
                    dve.wait_ge(y_read, 1 + g + 1)
                    if not last:
                        first_scores(g + 1)
                    moments(x_all, g, mv3, link).then_inc(stats3_done, 1)
                    if not last:
                        gated(0, g + 1)
                        versions(2, g + 1)
                    dve.wait_ge(std3_done, g + 1)
                    scales(mv3, std3, rstd3, shift3, link).then_inc(scale3_ready, 1)
                    assert done[0] == (2 if last else STEPS), done

                versions_q(0, 0)
                first_scores(0)
                gated(0, 0)
                versions(2, 0)
                with dve.Fori(0, G - 1) as g:
                    body(g, False)
                body(G - 1, True)


            def general_masks():
                nc.vector.tensor_copy(mask[:, 0, :, :], causal)
                nc.vector.memset(mask[:, 1:, 1, :], 0)
                dve.wait_ge(iota_ready, 2)
                apart, test = y_sb[:, 2 * P:3 * P], y_sb[:, 3 * P:4 * P]
                xor = og[:, 3 * P:4 * P].bitcast(I32)
                chain(nc.vector.tensor_tensor(xor, it[:, 0, :], it[:, 1, :], ALU.bitwise_xor))
                chain(nc.vector.tensor_copy(apart, xor))
                for i, L in enumerate(LEVELS):
                    chain(nc.vector.tensor_scalar(test, apart, float(L), None, ALU.is_ge))
                    chain(nc.vector.scalar_tensor_tensor(out=test, in0=apart, scalar=float(2 * L), in1=test,
                                                         op0=ALU.is_lt, op1=ALU.mult))
                    for t in (0, 2):
                        last = nc.vector.tensor_tensor(mask[:, 1 + i, t, :], test, causal[:, t, :], ALU.mult)
                    chain(last)
                chain(nc.vector.tensor_scalar(test, apart, 32.0, None, ALU.is_ge))
                chain(nc.vector.scalar_tensor_tensor(out=test, in0=apart, scalar=0.0, in1=test,
                                                     op0=ALU.is_equal, op1=ALU.add))
                for t in (0, 2):
                    last = nc.vector.tensor_tensor(mask[:, 0, t, :], test, causal[:, t, :], ALU.mult)
                chain(last)

            small_logit = dve.value_load(narrow[0:1, 0:1], min_val=0, max_val=1)
            before_masks = step[0]
            with dve.If(small_logit):
                general_masks()
                groups(LEVELS)
            with dve.Else():
                step[0] = before_masks
                chain(nc.vector.tensor_copy(mask[:, 0, :, :], causal))
                groups([])


def experts(nc, sb_, sem_, out, x_all, u_all, ident, ffn_w, wr_sb, NT, G, TG):
    T = NT * P
    HR = 4
    K = E * FB
    ctx = ExitStack()
    with ctx:
        def sb(name, shape, dt=F32):
            return sb_(name, shape, dt, ctx)

        def sem(name):
            return sem_(name, ctx)

        xt = sb("xt", [P, T])
        xt_hi = sb("xt_hi", [P, T], F32R)
        xt_lo = sb("xt_lo", [P, T], F32R)
        lg = sb("lg", [P, NT, E])
        ex = sb("ex", [P, NT, E])
        cand = sb("cand", [P, NT, E])
        first = sb("first", [P, NT, E])
        second = sb("second", [P, NT, E])
        rest = sb("rest", [P, NT, E])
        red = sb("red", [P, NT])
        rank = sb("rank", [P, E])
        gates = sb("gates", [P, NT, 64], F32R)
        gates_t = sb("gates_t", [64, T], F32R)
        pick_f = sb("pick_f", [64, E, P])
        pick = sb("pick", [64, E, P], F32R)
        h = sb("h", [P, 2, GT])
        h_hi = sb("h_hi", [P, HR, GT], F32R)
        h_lo = sb("h_lo", [P, HR, GT], F32R)
        gb = sb("gb", [P, 2, GT])
        part = sb("part", [P, GT])
        acc = sb("acc", [P, GT])
        ps = ctx.enter_context(nc.psum_tensor("ps", [P, 8, 512], F32))
        Y, GB, TR = 4, 6, 7

        dve_step2 = sem("dve_step2")
        turned = sem("turned")
        xt_ready = sem("xt_ready")
        xt_high_ready = sem("xt_high_ready")
        xt_split = sem("xt_split")
        logits_done = sem("logits_done")
        centred = sem("centred")
        exp_done = sem("exp_done")
        rank_ready = sem("rank_ready")
        pick_ready = sem("pick_ready")
        pick_split = sem("pick_split")
        gates_ready = sem("gates_ready")
        gates_turned = sem("gates_turned")
        gates_t_ready = sem("gates_t_ready")
        h_full = sem("h_full")
        h_act = sem("h_act")
        h_split = sem("h_split")
        y_step = sem("y_step")
        gb_full = sem("gb_full")
        gb_turn = sem("gb_turn")
        gb_ready = sem("gb_ready")
        y_used = sem("y_used")
        acc_step = sem("acc_step")
        acc_turned = sem("acc_turned")
        out_ready = sem("out_ready")
        out_sent = sem("out_sent")
        block = ctx.enter_context(nc.Block())

        @block.sync
        def _(sp):
            ov = out.rearrange("(t p) d -> p t d", p=P)
            for g in range(G):
                sp.wait_ge(out_ready, g + 1)
                sp.dma_start(ov[:, g * TG:(g + 1) * TG, :], x_all[:, g * TG:(g + 1) * TG, :]).then_inc(out_sent, 16)
            sp.wait_ge(out_sent, 16 * G)

        @block.gpsimd
        def _(pool):
            for e in range(E):
                last = nc.gpsimd.memset(rank[:, e:e + 1], float(E - e))
            last.then_inc(rank_ready, 1)
            nc.gpsimd.memset(pick_f[:], 1.0).then_inc(pick_ready, 1)
            pool.wait_ge(pick_ready, 1)
            for k in range(2):
                rows = slice(32 * k, 32 * k + 32)
                nc.gpsimd.affine_select(out=pick_f[rows, :, :], in_=pick_f[rows, :, :], compare_op=ALU.is_equal,
                                        fill=0.0, base=0, pattern=[[-1, E], [0, P]],
                                        channel_multiplier=1).then_inc(pick_ready, 1)

        LAG = 3
        AHEAD_PE, AHEAD = 4, 6

        @block.scalar
        def _(act):
            def xt_high(g):
                nc.scalar.activation(xt_hi[:, g * GT:(g + 1) * GT], ps[:, g, :], ACT.Copy).then_inc(xt_high_ready, 1)

            for g in range(G):
                act.wait_ge(turned, g + 1)
                if g == 0:
                    xt_high(g)
                nc.scalar.activation(xt[:, g * GT:(g + 1) * GT], ps[:, g, :], ACT.Copy).then_inc(xt_ready, 1)
            def block_out(k, g):
                n = K * g + k
                k = k % K
                act.wait_ge(h_full, n + 1)
                act.wait_ge(h_split, n + 1)
                nc.scalar.activation(h[:, k % 2, :], ps[:, k % HR, :], ACT.Silu).then_inc(h_act, 1)
                act.wait_ge(y_step, n + 1)
                nc.scalar.activation(h_hi[:, k % HR, :], ps[:, k % HR, :], ACT.Silu).then_inc(h_act, 1)

            def expert_gates(k, g):
                e = k % K // FB
                m = E * g + k // FB
                act.wait_ge(gb_full, m + 1)
                act.wait_ge(y_used, m + 1)
                nc.scalar.activation(gb[:, e % 2, :], ps[:, GB, :], ACT.Copy).then_inc(gb_ready, 1)

            for k in range(LAG):
                block_out(k, 0)
            act.wait_ge(centred, 1)
            nc.scalar.activation(ex[:], lg[:], ACT.Exp).then_inc(exp_done, 1)
            for k in range(LAG, AHEAD):
                block_out(k, 0)
            for g in range(G):
                act.wait_ge(gates_turned, g + 1)
                nc.scalar.activation(gates_t[:, g * GT:(g + 1) * GT], ps[0:64, (Y + 1, TR)[g % 2], :], ACT.Copy)\
                  .then_inc(gates_t_ready, 1)
            act.sem_inc(gb_ready, 1)
            expert_gates(FB - 1, 0)

            def body(g, last):
                for k in range(AHEAD, K if last else K + AHEAD):
                    block_out(k, g)
                    if k % FB == FB - 1:
                        expert_gates(k, g)

            with act.Fori(0, G - 1) as g:
                body(g, False)
            body(G - 1, True)

        @block.tensor
        def _(pe):
            def three(dst, w_hi, w_lo, x_hi, x_lo, start=True, stop=True):
                nc.tensor.matmul(dst, w_hi, x_hi, start=start, stop=False)
                nc.tensor.matmul(dst, w_hi, x_lo, start=False, stop=False)
                return nc.tensor.matmul(dst, w_lo, x_hi, start=False, stop=stop)

            def cols(g):
                return bass.ds(g * GT, GT)

            def hidden(k, g):
                g = g + k // K
                k = k % K
                e, f = divmod(k, FB)
                three(ps[:, k % HR, :], ffn_w[0][:, e, f, :], ffn_w[1][:, e, f, :], xt_hi[:, cols(g)],
                      xt_lo[:, cols(g)]).then_inc(h_full, 1)

            def spread_gates(k, g):
                g = g + k // K
                e = k % K // FB
                pe.wait_ge(gb_ready, E * g + e + 1)
                pe.sem_inc(gb_turn, 1)
                nc.tensor.matmul(ps[:, GB, :], pick[:, e, :], gates_t[:, cols(g)], start=True, stop=True)\
                  .then_inc(gb_full, 1)

            def back(k, g):
                g = g + k // K
                k = k % K
                e, f = divmod(k, FB)
                if f == 0:
                    pe.wait_ge(y_used, E * g + e + 1)
                pe.wait_ge(h_split, 2 + K * g + k + 1)
                three(ps[:, Y + e % 2, :], ffn_w[2][:, e, f, :], ffn_w[3][:, e, f, :], h_hi[:, k % HR, :],
                      h_lo[:, k % HR, :], start=(f == 0), stop=(f == FB - 1)).then_inc(y_step, 1)

            for g in range(G):
                for t in range(TG):
                    mm = nc.tensor.transpose(ps[:, g, t * P:(t + 1) * P], u_all[:, g * TG + t, :], ident[:])
                mm.then_inc(turned, 1)
            pe.sem_inc(y_step, HR)
            pe.wait_ge(xt_split, 1)
            for k in range(LAG):
                pe.wait_ge(xt_ready, k + 1)
                hidden(k, 0)
            for g in range(G):
                pe.wait_ge(xt_ready, g + 1)
                for t in range(g * TG, (g + 1) * TG):
                    mm = nc.tensor.matmul(ps[:, TR, t * E:(t + 1) * E], xt[:, t * P:(t + 1) * P], wr_sb[:],
                                          start=True, stop=True)
            mm.then_inc(logits_done, 1)
            for k in range(AHEAD_PE):
                hidden(k + LAG, 0)
                back(k, 0)
            pe.wait_ge(gates_ready, 1)
            for g in range(G):
                if g >= 2:
                    pe.wait_ge(gates_t_ready, g - 1)
                for t in range(TG):
                    mm = nc.tensor.transpose(ps[0:64, (Y + 1, TR)[g % 2], t * P:(t + 1) * P],
                                             gates[:, g * TG + t, :].bitcast(F32), ident[:])
                mm.then_inc(gates_turned, 1)
            pe.wait_ge(pick_split, 1)
            spread_gates(FB - 1, 0)
            pe.wait_ge(gates_t_ready, G)

            def body(g, last):
                for k in range(AHEAD_PE, K if last else K + AHEAD_PE):
                    if k + LAG == K:
                        pe.wait_ge(xt_split, G)
                    if k + LAG < K or not last:
                        hidden(k + LAG, g)
                        if (k + LAG) % FB == FB - 1:
                            spread_gates(k + LAG, g)
                    back(k, g)
                pe.wait_ge(acc_step, E * (g + 1))
                for t in range(TG):
                    mm = nc.tensor.transpose(ps[:, TR, t * P:(t + 1) * P], acc[:, t * P:(t + 1) * P], ident[:])
                mm.then_inc(acc_turned, 1)

            with pe.Fori(0, G - 1) as g:
                body(g, False)
            body(G - 1, True)

        @block.vector
        def _(dve):
            step = [0]

            def chain(ins):
                step[0] += 1
                ins.then_inc(dve_step2, 1)
                dve.wait_ge(dve_step2, step[0])

            dve.wait_ge(rank_ready, 1)
            nc.vector.memset(gates[:].bitcast(F32), 0.0)
            dve.wait_ge(pick_ready, 3)
            nc.vector.tensor_copy(pick[:], pick_f[:]).then_inc(pick_split, 1)
            def split_xt(g):
                cols = slice(g * GT, (g + 1) * GT)
                dve.wait_ge(xt_ready, g + 1)
                if g == 0:
                    dve.wait_ge(xt_high_ready, 1)
                else:
                    chain(nc.vector.tensor_copy(xt_hi[:, cols], xt[:, cols]))
                nc.vector.tensor_tensor(xt_lo[:, cols], xt[:, cols], xt_hi[:, cols].bitcast(F32), ALU.subtract)\
                  .then_inc(xt_split, 1)

            def low(k, g):
                n = K * g + k
                k = k % K
                dve.wait_ge(h_act, 2 * n + 2)
                nc.vector.tensor_tensor(h_lo[:, k % HR, :], h[:, k % 2, :], h_hi[:, k % HR, :].bitcast(F32),
                                        ALU.subtract).then_inc(h_split, 1)

            dve.sem_inc(h_split, 2)
            dve.sem_inc(y_used, 2)
            split_xt(0)

            def wide(a):
                return a[:].unsqueeze(2).to_broadcast([P, NT, E])

            ranks = rank[:].unsqueeze(1).to_broadcast([P, NT, E])

            def largest(src, hot):
                chain(nc.vector.tensor_reduce(red[:], src, AX.X, ALU.max))
                chain(nc.vector.tensor_tensor(cand[:], src, wide(red), ALU.is_equal))
                chain(nc.vector.tensor_tensor(cand[:], cand[:], ranks, ALU.mult))
                chain(nc.vector.tensor_reduce(red[:], cand[:], AX.X, ALU.max))
                chain(nc.vector.tensor_tensor(hot[:], cand[:], wide(red), ALU.is_equal))

            for k in range(LAG):
                low(k, 0)
            dve.wait_ge(logits_done, 1)
            logits = ps[:, TR, 0:NT * E].rearrange("p (t e) -> p t e", e=E)
            chain(nc.vector.tensor_reduce(red[:], logits, AX.X, ALU.max))
            nc.vector.tensor_tensor(lg[:], logits, wide(red), ALU.subtract).then_inc(centred, 1)
            dve.wait_ge(centred, 1)
            largest(lg[:], first)
            low(LAG, 0)
            chain(nc.vector.scalar_tensor_tensor(out=rest[:], in0=first[:], scalar=NEG, in1=lg[:], op0=ALU.mult,
                                                 op1=ALU.add))
            largest(rest[:], second)
            chain(nc.vector.tensor_tensor(first[:], first[:], second[:], ALU.add))
            dve.wait_ge(exp_done, 1)
            chain(nc.vector.tensor_tensor(first[:], first[:], ex[:], ALU.mult))
            chain(nc.vector.tensor_reduce(red[:], first[:], AX.X, ALU.add))
            chain(nc.vector.reciprocal(red[:], red[:]))
            chain(nc.vector.tensor_tensor(first[:], first[:], wide(red), ALU.mult))
            chain(nc.vector.tensor_copy(gates[:, :, 0:E], first[:]))
            nc.vector.tensor_tensor(gates[:, :, 32:32 + E], first[:], gates[:, :, 0:E].bitcast(F32),
                                    ALU.subtract).then_inc(gates_ready, 1)
            for k in range(HR, AHEAD):
                low(k, 0)
            for g in range(1, G):
                split_xt(g)

            def gather(g, e):
                m = E * g + e
                dve.wait_ge(y_step, HR + FB * (m + 1))
                dve.wait_ge(gb_ready, 1 + m + 1)
                y = ps[:, Y + e % 2, :]
                if e == 0:
                    nc.vector.tensor_tensor(acc[:], y, gb[:, e % 2, :], ALU.mult).then_inc(y_used, 1)
                    dve.wait_ge(y_used, 2 + m + 1)
                    dve.sem_inc(acc_step, 1)
                else:
                    nc.vector.tensor_tensor(part[:], y, gb[:, e % 2, :], ALU.mult).then_inc(y_used, 1)
                    dve.wait_ge(y_used, 2 + m + 1)
                    nc.vector.tensor_tensor(acc[:], acc[:], part[:], ALU.add).then_inc(acc_step, 1)
                    dve.wait_ge(acc_step, m + 1)

            def body(g, last):
                for k in range(AHEAD, K if last else K + AHEAD):
                    low(k, g)
                    if k % FB == AHEAD % FB:
                        gather(g, (k - AHEAD) // FB)
                if last:
                    gather(g, E - 1)
                dve.wait_ge(acc_turned, g + 1)
                rows = bass.ds(g * TG, TG)
                nc.vector.tensor_tensor(x_all[:, rows, :], ps[:, TR, :].rearrange("p (t d) -> p t d", t=TG),
                                        x_all[:, rows, :], ALU.add).then_inc(out_ready, 1)

            with dve.Fori(0, G - 1) as g:
                body(g, False)
            body(G - 1, True)


def kernel(**inputs):
    import numpy as np
    import concourse.bacc as bacc
    from concourse.bass_utils import run_bass_kernel_spmd

    a = {k.replace("L0_attn_", "").replace("L0_ffn_", ""): np.asarray(v) for k, v in inputs.items()}
    by_channel = lambda v: v.reshape(PAIRS, P).T
    arrays = {
        "x": a["x"].reshape(-1, D),
        "w_in": np.concatenate([a[n].T for n in ("WQ", "WK", "Wg", "WV")], axis=1),
        "w_out": a["WO"].T.reshape(PAIRS, P, D).transpose(1, 0, 2).reshape(P, CH),
        "b_in": np.stack([by_channel(a[n]) for n in ("bQ", "bK", "bg")], axis=1),
        "b_v": a["bV"].reshape(1, CH),
        "cols": np.stack([a["bO"], a["ln_gamma"], a["ln_beta"]], axis=1),
        "alpha": by_channel(a["alpha_logit"].reshape(-1)),
        "alpha_row": a["alpha_logit"].reshape(1, CH),
        "w1": a["W1"].transpose(2, 0, 1).reshape(D, E * DFF),
        "w2": a["W2"].reshape(E, D, FB, P).transpose(3, 0, 2, 1).reshape(P, E * DFF),
        "w_router": a["Wr"].T,
    }
    arrays = {f"in_{k}": np.ascontiguousarray(v) for k, v in arrays.items()}
    nc = bacc.Bacc("TRN2", target_bir_lowering=False, num_devices=1)
    args = [nc.dram_tensor(n, v.shape, mybir.dt.from_np(v.dtype), kind="ExternalInput").ap()
            for n, v in arrays.items()]
    out = nc.dram_tensor("out_0", arrays["in_x"].shape, F32, kind="ExternalOutput").ap()
    build(nc, *args, out)
    r = run_bass_kernel_spmd(nc, [arrays], core_ids=[0])
    return r.results[0]["out_0"].reshape(a["x"].shape)
```
